# Optimizing a Trainium2 kernel written in Bass

```python
import numpy as np
import jax
import jax.numpy as jnp

def _softmax(x, axis=-1):
    return jax.nn.softmax(x, axis=axis)

def _gelu(x):
    return jax.nn.gelu(x, approximate=True)

def _silu(x):
    return jax.nn.silu(x)

def _sigmoid(x):
    return jax.nn.sigmoid(x)

def _layernorm(x, axis=-1, eps=1e-05):
    m = jnp.mean(x, axis=axis, keepdims=True)
    v = jnp.var(x, axis=axis, keepdims=True)
    return (x - m) / jnp.sqrt(v + eps)

def _scatter_add(tgt, idx, src, axis=0):
    return tgt.at[idx].add(src)

def _segment_sum(src, seg, n):
    return jax.ops.segment_sum(src, seg, n)
kernel_name = 'mk_conv_seq_d4_conv_nhwc256_r2_38a86e'

def setup_inputs(seed: int=0):
    np.random.seed(seed)
    _w = jnp.asarray

    def _rec_inputs():
        import jax
        import jax.numpy as jnp
        _gk = jax.random.key(seed)
        x = -0.000125 + 0.9999 * jax.random.normal(jax.random.fold_in(_gk, 1), (64, 32, 32, 128), jnp.float32)
        return x
    x = _rec_inputs()

    def _L0_conv_setup():
        import jax, jax.numpy as jnp
        import numpy as np
        H, W, C, HID, K = (32, 32, 128, 256, 1)

        def spiral_indices(h, w):
            cy, cx = (h // 2, w // 2)
            seen, seq = (set(), [])

            def add(y, x):
                if 0 <= y < h and 0 <= x < w and ((y, x) not in seen):
                    seen.add((y, x))
                    seq.append((y, x))
            add(cy, cx)
            max_r = max(cy, h - 1 - cy, cx, w - 1 - cx)
            for r in range(1, max_r + 1):
                top, bot, left, right = (cy - r, cy + r, cx - r, cx + r)
                for x in range(left, right + 1):
                    add(top, x)
                for y in range(top + 1, bot + 1):
                    add(y, right)
                for x in range(right - 1, left - 1, -1):
                    add(bot, x)
                for y in range(bot - 1, top, -1):
                    add(y, left)
            if len(seq) != h * w:
                for y in range(h):
                    for x in range(w):
                        add(y, x)
            return seq

        def _static(h, w):
            path = spiral_indices(h, w)
            n = len(path)
            pidx = np.zeros(n, np.int32)
            nidx = np.zeros((n, 4), np.int32)
            nmask = np.zeros((n, 4), np.float32)
            ncnt = np.zeros(n, np.float32)
            for i, (y, x) in enumerate(path):
                pidx[i] = y * w + x
                cands = [(y - 1, x), (y + 1, x), (y, x - 1), (y, x + 1)]
                j = 0
                for yy, xx in cands:
                    if 0 <= yy < h and 0 <= xx < w:
                        nidx[i, j] = yy * w + xx
                        nmask[i, j] = 1.0
                        j += 1
                ncnt[i] = max(j, 1)
            return (jnp.asarray(pidx), jnp.asarray(nidx), jnp.asarray(nmask), jnp.asarray(ncnt))
        key = jax.random.key(seed)
        k0, k1, k2, k3 = jax.random.split(key, 4)
        B = 64
        x = jax.random.normal(k0, (B, H, W, C), dtype=jnp.float32)
        w1 = jax.random.normal(k1, (2 * C, HID), dtype=jnp.float32) * 0.05
        b1 = jnp.zeros((HID,), jnp.float32)
        w2 = jax.random.normal(k2, (HID,), dtype=jnp.float32) * 0.05
        b2 = jnp.zeros((), jnp.float32)
        w_y = jax.random.normal(k3, (C,), dtype=jnp.float32) * 0.05
        return {'x': x, 'w1': w1, 'b1': b1, 'w2': w2, 'b2': b2, 'w_y': w_y}
    _L0_conv_all = _L0_conv_setup()
    _L0_conv_in = {k: v for k, v in _L0_conv_all.items() if k in ('w1', 'b1', 'w2', 'b2', 'w_y')}
    del _L0_conv_all

    def _L1_conv_setup():
        import jax, jax.numpy as jnp
        import numpy as np
        C = 128
        CQK = C // 8
        key = jax.random.key(seed)
        ks = jax.random.split(key, 8)
        B, H, W = (4, 32, 32)
        inputs = jax.random.normal(ks[0], (B, H, W, C), dtype=jnp.float32)
        s = 1.0 / np.sqrt(C)
        Wq = jax.random.normal(ks[1], (C, CQK), dtype=jnp.float32) * s
        bq = jnp.zeros((CQK,), dtype=jnp.float32)
        Wk = jax.random.normal(ks[2], (C, CQK), dtype=jnp.float32) * s
        bk = jnp.zeros((CQK,), dtype=jnp.float32)
        Wv = jax.random.normal(ks[3], (C, C), dtype=jnp.float32) * s
        bv = jnp.zeros((C,), dtype=jnp.float32)
        gamma = jnp.float32(0.7)
        return {'inputs': inputs, 'Wq': Wq, 'bq': bq, 'Wk': Wk, 'bk': bk, 'Wv': Wv, 'bv': bv, 'gamma': gamma}
    _L1_conv_all = _L1_conv_setup()
    _L1_conv_in = {k: v for k, v in _L1_conv_all.items() if k in ('Wq', 'bq', 'Wk', 'bk', 'Wv', 'bv', 'gamma')}
    del _L1_conv_all

    def _L2_conv_setup():
        import jax, jax.numpy as jnp
        import numpy as np
        key = jax.random.key(seed)
        ks = jax.random.split(key, 4)
        B, H, W, C = (4, 32, 32, 128)
        d = C // 8
        x = jax.random.normal(ks[0], (B, H, W, C), dtype=jnp.float32)
        wq = jax.random.normal(ks[1], (C, d), dtype=jnp.float32) * (1.0 / np.sqrt(C))
        wk = jax.random.normal(ks[2], (C, d), dtype=jnp.float32) * (1.0 / np.sqrt(C))
        wv = jax.random.normal(ks[3], (C, C), dtype=jnp.float32) * (1.0 / np.sqrt(C))
        bq = jnp.zeros((d,), dtype=jnp.float32)
        bk = jnp.zeros((d,), dtype=jnp.float32)
        bv = jnp.zeros((C,), dtype=jnp.float32)
        return {'x': x, 'wq': wq, 'bq': bq, 'wk': wk, 'bk': bk, 'wv': wv, 'bv': bv}
    _L2_conv_all = _L2_conv_setup()
    _L2_conv_in = {k: v for k, v in _L2_conv_all.items() if k in ('wq', 'bq', 'wk', 'bk', 'wv', 'bv')}
    del _L2_conv_all

    def _L3_conv_setup():
        import jax, jax.numpy as jnp
        import numpy as np
        H, W, C, HID, K = (32, 32, 128, 256, 1)

        def spiral_indices(h, w):
            cy, cx = (h // 2, w // 2)
            seen, seq = (set(), [])

            def add(y, x):
                if 0 <= y < h and 0 <= x < w and ((y, x) not in seen):
                    seen.add((y, x))
                    seq.append((y, x))
            add(cy, cx)
            max_r = max(cy, h - 1 - cy, cx, w - 1 - cx)
            for r in range(1, max_r + 1):
                top, bot, left, right = (cy - r, cy + r, cx - r, cx + r)
                for x in range(left, right + 1):
                    add(top, x)
                for y in range(top + 1, bot + 1):
                    add(y, right)
                for x in range(right - 1, left - 1, -1):
                    add(bot, x)
                for y in range(bot - 1, top, -1):
                    add(y, left)
            if len(seq) != h * w:
                for y in range(h):
                    for x in range(w):
                        add(y, x)
            return seq

        def _static(h, w):
            path = spiral_indices(h, w)
            n = len(path)
            pidx = np.zeros(n, np.int32)
            nidx = np.zeros((n, 4), np.int32)
            nmask = np.zeros((n, 4), np.float32)
            ncnt = np.zeros(n, np.float32)
            for i, (y, x) in enumerate(path):
                pidx[i] = y * w + x
                cands = [(y - 1, x), (y + 1, x), (y, x - 1), (y, x + 1)]
                j = 0
                for yy, xx in cands:
                    if 0 <= yy < h and 0 <= xx < w:
                        nidx[i, j] = yy * w + xx
                        nmask[i, j] = 1.0
                        j += 1
                ncnt[i] = max(j, 1)
            return (jnp.asarray(pidx), jnp.asarray(nidx), jnp.asarray(nmask), jnp.asarray(ncnt))
        key = jax.random.key(seed)
        k0, k1, k2, k3 = jax.random.split(key, 4)
        B = 64
        x = jax.random.normal(k0, (B, H, W, C), dtype=jnp.float32)
        w1 = jax.random.normal(k1, (2 * C, HID), dtype=jnp.float32) * 0.05
        b1 = jnp.zeros((HID,), jnp.float32)
        w2 = jax.random.normal(k2, (HID,), dtype=jnp.float32) * 0.05
        b2 = jnp.zeros((), jnp.float32)
        w_y = jax.random.normal(k3, (C,), dtype=jnp.float32) * 0.05
        return {'x': x, 'w1': w1, 'b1': b1, 'w2': w2, 'b2': b2, 'w_y': w_y}
    _L3_conv_all = _L3_conv_setup()
    _L3_conv_in = {k: v for k, v in _L3_conv_all.items() if k in ('w1', 'b1', 'w2', 'b2', 'w_y')}
    del _L3_conv_all
    return {'x': x, 'L0_conv_w1': _L0_conv_in['w1'], 'L0_conv_b1': _L0_conv_in['b1'], 'L0_conv_w2': _L0_conv_in['w2'], 'L0_conv_b2': _L0_conv_in['b2'], 'L0_conv_w_y': _L0_conv_in['w_y'], 'L1_conv_Wq': _L1_conv_in['Wq'], 'L1_conv_bq': _L1_conv_in['bq'], 'L1_conv_Wk': _L1_conv_in['Wk'], 'L1_conv_bk': _L1_conv_in['bk'], 'L1_conv_Wv': _L1_conv_in['Wv'], 'L1_conv_bv': _L1_conv_in['bv'], 'L1_conv_gamma': _L1_conv_in['gamma'], 'L2_conv_wq': _L2_conv_in['wq'], 'L2_conv_bq': _L2_conv_in['bq'], 'L2_conv_wk': _L2_conv_in['wk'], 'L2_conv_bk': _L2_conv_in['bk'], 'L2_conv_wv': _L2_conv_in['wv'], 'L2_conv_bv': _L2_conv_in['bv'], 'L3_conv_w1': _L3_conv_in['w1'], 'L3_conv_b1': _L3_conv_in['b1'], 'L3_conv_w2': _L3_conv_in['w2'], 'L3_conv_b2': _L3_conv_in['b2'], 'L3_conv_w_y': _L3_conv_in['w_y']}

def reference(x, L0_conv_w1, L0_conv_b1, L0_conv_w2, L0_conv_b2, L0_conv_w_y, L1_conv_Wq, L1_conv_bq, L1_conv_Wk, L1_conv_bk, L1_conv_Wv, L1_conv_bv, L1_conv_gamma, L2_conv_wq, L2_conv_bq, L2_conv_wk, L2_conv_bk, L2_conv_wv, L2_conv_bv, L3_conv_w1, L3_conv_b1, L3_conv_w2, L3_conv_b2, L3_conv_w_y):
    import jax
    import jax.numpy as jnp

    def _L0_conv_ref(x, w1, b1, w2, b2, w_y):
        import jax, jax.numpy as jnp
        import numpy as np
        H, W, C, HID, K = (32, 32, 128, 256, 1)

        def spiral_indices(h, w):
            cy, cx = (h // 2, w // 2)
            seen, seq = (set(), [])

            def add(y, x):
                if 0 <= y < h and 0 <= x < w and ((y, x) not in seen):
                    seen.add((y, x))
                    seq.append((y, x))
            add(cy, cx)
            max_r = max(cy, h - 1 - cy, cx, w - 1 - cx)
            for r in range(1, max_r + 1):
                top, bot, left, right = (cy - r, cy + r, cx - r, cx + r)
                for x in range(left, right + 1):
                    add(top, x)
                for y in range(top + 1, bot + 1):
                    add(y, right)
                for x in range(right - 1, left - 1, -1):
                    add(bot, x)
                for y in range(bot - 1, top, -1):
                    add(y, left)
            if len(seq) != h * w:
                for y in range(h):
                    for x in range(w):
                        add(y, x)
            return seq

        def _static(h, w):
            path = spiral_indices(h, w)
            n = len(path)
            pidx = np.zeros(n, np.int32)
            nidx = np.zeros((n, 4), np.int32)
            nmask = np.zeros((n, 4), np.float32)
            ncnt = np.zeros(n, np.float32)
            for i, (y, x) in enumerate(path):
                pidx[i] = y * w + x
                cands = [(y - 1, x), (y + 1, x), (y, x - 1), (y, x + 1)]
                j = 0
                for yy, xx in cands:
                    if 0 <= yy < h and 0 <= xx < w:
                        nidx[i, j] = yy * w + xx
                        nmask[i, j] = 1.0
                        j += 1
                ncnt[i] = max(j, 1)
            return (jnp.asarray(pidx), jnp.asarray(nidx), jnp.asarray(nmask), jnp.asarray(ncnt))
        B, h, w, c = x.shape
        pidx, nidx, nmask, ncnt = _static(h, w)
        g = x.reshape(B, h * w, c)

        def step(g, inp):
            ci, ni, nm, nc = inp
            local = g[:, ci, :]
            nb = g[:, ni, :]
            neigh = (nb * nm[None, :, None]).sum(axis=1) / nc
            u = jnp.concatenate([local, neigh], axis=-1)
            y_sc = jnp.tanh(u @ w1 + b1) @ w2 + b2
            g = g.at[:, ci, :].set(local + y_sc[:, None] * w_y[None, :])
            return (g, None)
        for _ in range(K):
            g, _ = jax.lax.scan(step, g, (pidx, nidx, nmask, ncnt))
        return g.reshape(B, h, w, c)

    def _L1_conv_ref(inputs, Wq, bq, Wk, bk, Wv, bv, gamma):
        import jax, jax.numpy as jnp
        import numpy as np
        C = 128
        CQK = C // 8
        B, H, W, Cin = inputs.shape
        N = H * W
        x = inputs.reshape(B, N, Cin)
        q = x @ Wq + bq
        k = x @ Wk + bk
        v = x @ Wv + bv
        energy = jnp.einsum('bnd,bmd->bnm', q, k)
        attn = jax.nn.softmax(energy, axis=-1)
        x_out = jnp.einsum('bnm,bmc->bnc', attn, v)
        out = gamma * x_out.reshape(B, H, W, Cin) + inputs
        return out

    def _L2_conv_ref(x, wq, bq, wk, bk, wv, bv):
        import jax, jax.numpy as jnp
        import numpy as np
        B, H, W, C = x.shape
        N = H * W
        xf = x.reshape(B, N, C)
        q = xf @ wq + bq
        k = xf @ wk + bk
        v = xf @ wv + bv
        attn = jax.nn.softmax(jnp.einsum('bnd,bmd->bnm', q, k), axis=-1)
        out = jnp.einsum('bnm,bmc->bnc', attn, v)
        return out.reshape(B, H, W, C) + x

    def _L3_conv_ref(x, w1, b1, w2, b2, w_y):
        import jax, jax.numpy as jnp
        import numpy as np
        H, W, C, HID, K = (32, 32, 128, 256, 1)

        def spiral_indices(h, w):
            cy, cx = (h // 2, w // 2)
            seen, seq = (set(), [])

            def add(y, x):
                if 0 <= y < h and 0 <= x < w and ((y, x) not in seen):
                    seen.add((y, x))
                    seq.append((y, x))
            add(cy, cx)
            max_r = max(cy, h - 1 - cy, cx, w - 1 - cx)
            for r in range(1, max_r + 1):
                top, bot, left, right = (cy - r, cy + r, cx - r, cx + r)
                for x in range(left, right + 1):
                    add(top, x)
                for y in range(top + 1, bot + 1):
                    add(y, right)
                for x in range(right - 1, left - 1, -1):
                    add(bot, x)
                for y in range(bot - 1, top, -1):
                    add(y, left)
            if len(seq) != h * w:
                for y in range(h):
                    for x in range(w):
                        add(y, x)
            return seq

        def _static(h, w):
            path = spiral_indices(h, w)
            n = len(path)
            pidx = np.zeros(n, np.int32)
            nidx = np.zeros((n, 4), np.int32)
            nmask = np.zeros((n, 4), np.float32)
            ncnt = np.zeros(n, np.float32)
            for i, (y, x) in enumerate(path):
                pidx[i] = y * w + x
                cands = [(y - 1, x), (y + 1, x), (y, x - 1), (y, x + 1)]
                j = 0
                for yy, xx in cands:
                    if 0 <= yy < h and 0 <= xx < w:
                        nidx[i, j] = yy * w + xx
                        nmask[i, j] = 1.0
                        j += 1
                ncnt[i] = max(j, 1)
            return (jnp.asarray(pidx), jnp.asarray(nidx), jnp.asarray(nmask), jnp.asarray(ncnt))
        B, h, w, c = x.shape
        pidx, nidx, nmask, ncnt = _static(h, w)
        g = x.reshape(B, h * w, c)

        def step(g, inp):
            ci, ni, nm, nc = inp
            local = g[:, ci, :]
            nb = g[:, ni, :]
            neigh = (nb * nm[None, :, None]).sum(axis=1) / nc
            u = jnp.concatenate([local, neigh], axis=-1)
            y_sc = jnp.tanh(u @ w1 + b1) @ w2 + b2
            g = g.at[:, ci, :].set(local + y_sc[:, None] * w_y[None, :])
            return (g, None)
        for _ in range(K):
            g, _ = jax.lax.scan(step, g, (pidx, nidx, nmask, ncnt))
        return g.reshape(B, h, w, c)

    def _gn(v, G=32, eps=1e-05):
        B_, H_, W_, C_ = v.shape
        g = v.reshape(B_, H_, W_, G, C_ // G)
        m = jnp.mean(g, axis=(1, 2, 4), keepdims=True)
        s = jnp.var(g, axis=(1, 2, 4), keepdims=True)
        return ((g - m) / jnp.sqrt(s + eps)).reshape(v.shape)

    def _ln_c(v, eps=1e-06):
        m = jnp.mean(v, axis=-1, keepdims=True)
        s = jnp.var(v, axis=-1, keepdims=True)
        return (v - m) / jnp.sqrt(s + eps)

    def _ln_t(v, eps=1e-05):
        m = jnp.mean(v, axis=-1, keepdims=True)
        s = jnp.var(v, axis=-1, keepdims=True)
        return (v - m) / jnp.sqrt(s + eps)

    def _to_tokens(v):
        B_, H_, W_, C_ = v.shape
        return v.reshape(B_, H_ * W_, C_)

    def _from_tokens(t, like):
        return t.reshape(like.shape)
    x = _L0_conv_ref(x, L0_conv_w1, L0_conv_b1, L0_conv_w2, L0_conv_b2, L0_conv_w_y)
    x = _L1_conv_ref(x, L1_conv_Wq, L1_conv_bq, L1_conv_Wk, L1_conv_bk, L1_conv_Wv, L1_conv_bv, L1_conv_gamma)
    x = _L2_conv_ref(x, L2_conv_wq, L2_conv_bq, L2_conv_wk, L2_conv_bk, L2_conv_wv, L2_conv_bv)
    x = _L3_conv_ref(x, L3_conv_w1, L3_conv_b1, L3_conv_w2, L3_conv_b2, L3_conv_w_y)
    return x

_drawn_inputs = setup_inputs


def setup_inputs(seed=0):
    import zlib

    import numpy as np

    out = dict(_drawn_inputs(seed))
    spreads = {'L0_conv_b1': (0.0, 0.727),
     'L1_conv_bq': (0.0, 0.1),
     'L1_conv_bk': (0.0, 0.8),
     'L1_conv_bv': (0.0, 0.1),
     'L2_conv_bq': (0.0, 0.1),
     'L2_conv_bk': (0.0, 0.8),
     'L2_conv_bv': (0.0, 0.1),
     'L3_conv_b1': (0.0, 0.8)}
    factors = {'L3_conv_w1': 3.36, 'L3_conv_w2': 2.895, 'L3_conv_w_y': 3.074}
    for name, (base, spread) in spreads.items():
        noise = np.random.default_rng([zlib.crc32(name.encode()), seed]).standard_normal(out[name].shape)
        drawn = base * np.exp(spread * noise) if base else spread * noise
        out[name] = jnp.asarray(drawn.astype(out[name].dtype))
    for name, factor in factors.items():
        out[name] = (out[name] * factor).astype(out[name].dtype)
    return out
```

```python
from contextlib import ExitStack

import numpy as np

import concourse.bass as bass
from concourse import mybir

F32 = mybir.dt.float32
F32R = mybir.dt.float32r
ALU = mybir.AluOpType
ACT = mybir.ActivationFunctionType
AX_X = mybir.AxisListType.X

P = 128
SIDE = 32
CELLS = SIDE * SIDE
BATCH = 64
HID = 256
DQK = 16
BANK = 512



def spiral_path():
    cy = cx = SIDE // 2
    path, seen = [], set()

    def visit(ring, y, x):
        if 0 <= y < SIDE and 0 <= x < SIDE and (y, x) not in seen:
            seen.add((y, x))
            path.append((ring, y, x))

    visit(0, cy, cx)
    for r in range(1, SIDE // 2 + 1):
        top, bottom, left, right = cy - r, cy + r, cx - r, cx + r
        for x in range(left, right + 1):
            visit(r, top, x)
        for y in range(top + 1, bottom + 1):
            visit(r, y, right)
        for x in range(right - 1, left - 1, -1):
            visit(r, bottom, x)
        for y in range(bottom - 1, top, -1):
            visit(r, y, left)
    return path


LATE, OLD, NEW = range(3)


def neighbours(y, x):
    near = ((y - 1, x), (y + 1, x), (y, x - 1), (y, x + 1))
    return [(a, b) for a, b in near if 0 <= a < SIDE and 0 <= b < SIDE]


def wavefront():
    path = spiral_path()
    rank = {(y, x): n for n, (_, y, x) in enumerate(path)}
    level, ring = {}, {}
    for n, (r, y, x) in enumerate(path):
        earlier = [level[c] for c in neighbours(y, x) if rank[c] < n]
        level[y, x] = max(earlier, default=-1 if (y, x) != (0, 0) else 0) + 1
        ring[y, x] = r
    order = sorted(level, key=lambda c: (level[c], ring[c]))
    at = {c: n for n, c in enumerate(order)}
    starts = [0]
    for n, c in enumerate(order):
        if level[c] == len(starts):
            starts.append(n)
    starts.append(CELLS)

    sums_late, sums_old, sums_new, edges, last_read = [], [], [], [], [0] * CELLS
    for lv in range(len(starts) - 1):
        late_ops, old_ops, new_ops, edge_runs = [], [], [], []

        def run(ops, key, n, a, b):
            if ops and ops[-1][0] == key:
                _, n0, k, a0, b0 = ops[-1]
                follows = all((s is None) == (s0 is None) and (s is None or s == s0 + k)
                              for s, s0 in ((a, a0), (b, b0)))
                if n == n0 + k and follows:
                    ops[-1] = (key, n0, k + 1, a0, b0)
                    return
            ops.append((key, n, 1, a, b))

        by_turn = {}
        for n in range(starts[lv], starts[lv + 1]):
            c = order[n]
            near = neighbours(*c)
            late = sorted((at[d] for d in near if rank[d] > rank[c]), reverse=True)
            early = sorted(at[d] for d in near if rank[d] < rank[c])
            before = [a for a in early if rank[order[a]] == rank[c] - 1]
            early = [a for a in early if a not in before]
            assert all(level[order[a]] < lv for a in early + before)
            assert all(level[order[a]] > lv for a in late)
            for a in early + before:
                last_read[a] = max(last_read[a], lv)
            new = [a for a in early if level[order[a]] == lv - 1]
            old = [a for a in early if level[order[a]] < lv - 1]
            terms = ([(a, LATE, t) for t, a in enumerate(late)] + [(a, OLD, t) for t, a in enumerate(old)]
                     + [(a, NEW, t) for t, a in enumerate(new)] + [(a, NEW, 9) for a in before])
            (a, _, _), (b, kind, t) = terms[:2]
            by_turn.setdefault((kind, t), []).append((n, a, b))
            for a, kind, t in terms[2:]:
                by_turn.setdefault((kind, t), []).append((n, None, a))
            if len(near) < 4:
                run(edge_runs, len(near), n, None, None)
        ops = {LATE: late_ops, OLD: old_ops, NEW: new_ops}
        for (kind, turn), terms in sorted(by_turn.items()):
            for n, a, b in terms:
                run(ops[kind], turn, n, a, b)
        sums_late.append([o[1:] for o in late_ops])
        sums_old.append([o[1:] for o in old_ops])
        sums_new.append([o[1:] for o in new_ops])
        edges.append([(n, k, count) for count, n, k, _, _ in edge_runs])
    grid = np.array([y * SIDE + x for y, x in order])
    return grid, starts, sums_late, sums_old, sums_new, edges, last_read


GRID, STARTS, SUMS_LATE, SUMS_OLD, SUMS_NEW, EDGES, LAST_READ = wavefront()
LEVELS = len(STARTS) - 1


def chunk_levels():
    first = [0, 2]
    for lv in range(2, LEVELS):
        if STARTS[lv + 1] - STARTS[first[-1]] > CELLS // 8 and lv > first[-1]:
            first.append(lv)
    return first + [LEVELS]


CHUNKS = chunk_levels()


def positive(engine, semaphore, value):
    if not isinstance(value, int) or value > 0:
        engine.wait_ge(semaphore, value)



def scan_layer(nc, sems, tag, psum, src, dst, w1, b1, w2, b2, w_y):
    STREAMS = 2
    IMAGES = 16
    ROUNDS = BATCH // (STREAMS * IMAGES)
    HALVES = HID // P
    WIDE = max(b - a for a, b in zip(STARTS, STARTS[1:]))
    assert HALVES * WIDE * IMAGES <= BANK
    NC = len(CHUNKS) - 1

    with ExitStack() as ctx:
        sb = lambda name, shape, dt=F32: ctx.enter_context(nc.sbuf_tensor(f"{tag}_{name}", shape, dt))
        sem = lambda name: sems.enter_context(nc.semaphore(f"{tag}_{name}"))
        each = range(STREAMS)

        x = [sb(f"x{s}", [P, IMAGES, CELLS]) for s in each]
        near = [[sb(f"near{s}_{k}", [P, IMAGES, WIDE]) for k in range(2)] for s in each]
        hidden = [[sb(f"hidden{s}_{h}", [P, IMAGES, WIDE]) for h in range(HALVES)] for s in each]
        w1_own = sb("w1_own", [P, HID])
        w1_near = sb("w1_near", [P, HID])
        w1_sum = sb("w1_sum", [P, HID])
        b1_col = sb("b1_col", [P, HALVES])
        w2_col = sb("w2_col", [P, HALVES])
        wy_rows = sb("wy_rows", [P, P])
        wy_col = sb("wy_col", [P, 1])
        b2_col = sb("b2_col", [P, 1])
        b2wy = sb("b2wy", [P, 1])
        w2wy = [sb(f"w2wy{h}", [P, P]) for h in range(HALVES)]
        pre = [[psum[s][:, k * BANK:(k + 1) * BANK] for k in range(2)] for s in each]
        step = [psum[2 + s][:, 0:BANK] for s in each]

        weights_in = sem("weights_in")
        weights_ready = sem("weights_ready")
        loaded = [sem(f"loaded{k}") for k in range(NC)]
        stored = [sem(f"stored{k}") for k in range(NC)]
        late_ready = [sem(f"late_ready{s}") for s in each]
        near_ready = [sem(f"near_ready{s}") for s in each]
        pre_ready = [sem(f"pre_ready{s}") for s in each]
        tanh_ready = [sem(f"tanh_ready{s}") for s in each]
        step_ready = [sem(f"step_ready{s}") for s in each]
        updated = [sem(f"updated{s}") for s in each]
        own_done = [sem(f"own_done{s}") for s in each]
        near_turn = sem("near_turn")
        late_turn = sem("late_turn")
        block = ctx.enter_context(nc.Block())

        def images(r, s):
            return slice((r * STREAMS + s) * IMAGES, (r * STREAMS + s + 1) * IMAGES)

        def chunk(k):
            return slice(STARTS[CHUNKS[k]], STARTS[CHUNKS[k + 1]])

        def cells(t, lv):
            return t[:, :, 0:STARTS[lv + 1] - STARTS[lv]]

        def columns(t, lv, h=0):
            n = STARTS[lv + 1] - STARTS[lv]
            a = h * IMAGES * n
            return t[:, a:a + IMAGES * n].rearrange("p (b n) -> p b n", b=IMAGES)

        def late_count(lv):
            return sum(len(SUMS_LATE[v]) for v in range(lv))

        def turn_count(s, lv, new):
            early = [len(SUMS_OLD[v]) + len(SUMS_NEW[v]) + len(EDGES[v]) for v in range(lv + 1)]
            return STREAMS * sum(early[:lv]) + s * early[lv] + (len(SUMS_OLD[lv]) if new else 0)

        LATE_ROUND = late_count(LEVELS)
        TURN_ROUND = turn_count(STREAMS - 1, LEVELS - 1, True) + len(SUMS_NEW[-1]) + len(EDGES[-1])

        def reload(sp, r, k):
            last = max(LAST_READ[chunk(k)])
            sp.wait_ge(stored[k], 16 * STREAMS * (r + 1))
            for s in each:
                sp.wait_ge(near_ready[s], r * LEVELS + max(last + 1, CHUNKS[k + 1]))
                sp.dma_start(x[s][:, :, chunk(k)],
                             src[images(r + 1, s), :, chunk(k)].rearrange("b c n -> c b n")
                             ).then_inc(loaded[k], 16)

        @block.sync
        def _(sp):
            with nc.allow_non_contiguous_dma(reason="small weight columns"):
                for dram, tile in ((w1[0:P, :], w1_own[:]), (w1[P:2 * P, :], w1_near[:]),
                                   (b1.rearrange("(h p) -> p h", p=P), b1_col[:]),
                                   (w2.rearrange("(h p) -> p h", p=P), w2_col[:]),
                                   (w_y.rearrange("(a c) -> a c", a=1).to_broadcast([P, P]), wy_rows[:]),
                                   (w_y.rearrange("(c a) -> c a", a=1), wy_col[:]),
                                   (b2.to_broadcast([P, 1]), b2_col[:])):
                    sp.dma_start(tile, dram).then_inc(weights_in, 16)
                for k in range(NC):
                    for s in each:
                        sp.dma_start(x[s][:, :, chunk(k)],
                                     src[images(0, s), :, chunk(k)].rearrange("b c n -> c b n")
                                     ).then_inc(loaded[k], 16)
                for r in range(ROUNDS):
                    for k in range(NC):
                        for s in each:
                            sp.wait_ge(updated[s], r * LEVELS + CHUNKS[k + 1])
                            sp.dma_start(dst[images(r, s), :, chunk(k)].rearrange("b c n -> c b n"),
                                         x[s][:, :, chunk(k)]).then_inc(stored[k], 16)
                        if r + 1 < ROUNDS and k >= 2:
                            reload(sp, r, k - 1)
                    if r + 1 < ROUNDS:
                        reload(sp, r, NC - 1)
                        reload(sp, r, 0)
                for k in range(NC):
                    sp.wait_ge(stored[k], 16 * STREAMS * ROUNDS)

        @block.gpsimd
        def _(pool):
            with pool.Fori(0, ROUNDS) as r:
                for k in range(NC):
                    pool.wait_ge(loaded[k], 16 * STREAMS * (r + 1))
                for lv in range(LEVELS):
                    for s in each:
                        if lv >= 2:
                            pool.wait_ge(pre_ready[s], r * LEVELS + lv - 1)
                        for n, (a, k, s0, s1) in enumerate(SUMS_LATE[lv]):
                            o = a - STARTS[lv]
                            out = near[s][lv % 2][:, :, o:o + k]
                            if s0 is None:
                                pool.wait_ge(late_ready[s], r * LATE_ROUND + late_count(lv) + n)
                            in0 = out if s0 is None else x[s][:, :, s0:s0 + k]
                            nc.gpsimd.tensor_tensor(out, in0, x[s][:, :, s1:s1 + k], ALU.add
                                                    ).then_inc(late_ready[s], 1)

        @block.vector
        def _(dve):
            dve.wait_ge(weights_in, 16 * 7)
            nc.vector.tensor_scalar(w1_sum[:], w1_near[:], 0.25, None, ALU.mult).then_inc(weights_ready, 1)
            nc.vector.tensor_tensor(b2wy[:], b2_col[:], wy_col[:], ALU.mult).then_inc(weights_ready, 1)
            for h in range(HALVES):
                nc.vector.tensor_scalar(w2wy[h][:], wy_rows[:], w2_col[:, h:h + 1], None,
                                        ALU.mult).then_inc(weights_ready, 1)
            dve.wait_ge(weights_ready, 2 + HALVES)

            def add(s, lv, r, n, a, k, s0, s1):
                out = near[s][lv % 2][:, :, a - STARTS[lv]:a - STARTS[lv] + k]
                if s0 is None and n > 0:
                    dve.wait_ge(near_turn, r * TURN_ROUND + n)
                in0 = out if s0 is None else x[s][:, :, s0:s0 + k]
                return nc.vector.tensor_tensor(out, in0, x[s][:, :, s1:s1 + k], ALU.add
                                               ).then_inc(near_turn, 1)

            def old_neighbours(s, lv, r):
                dve.wait_ge(late_ready[s], r * LATE_ROUND + late_count(lv + 1))
                n = turn_count(s, lv, False)
                for m, op in enumerate(SUMS_OLD[lv]):
                    add(s, lv, r, n + m, *op)

            def new_neighbours(s, lv, r):
                n = turn_count(s, lv, True)
                for m, op in enumerate(SUMS_NEW[lv]):
                    add(s, lv, r, n + m, *op)
                n += len(SUMS_NEW[lv])
                for m, (a, k, count) in enumerate(EDGES[lv]):
                    out = near[s][lv % 2][:, :, a - STARTS[lv]:a - STARTS[lv] + k]
                    if n + m > 0:
                        dve.wait_ge(near_turn, r * TURN_ROUND + n + m)
                    nc.vector.tensor_scalar(out, out, 4.0 / count, None, ALU.mult).then_inc(near_turn, 1)
                n += len(EDGES[lv])
                if n > 0:
                    dve.wait_ge(near_turn, r * TURN_ROUND + n)
                dve.sem_inc(near_ready[s], 1)

            with dve.Fori(0, ROUNDS) as r:
                for s in each:
                    old_neighbours(s, 0, r)
                    new_neighbours(s, 0, r)
                for lv in range(LEVELS):
                    for s in each:
                        if lv + 1 < LEVELS:
                            old_neighbours(s, lv + 1, r)
                        dve.wait_ge(step_ready[s], r * LEVELS + lv + 1)
                        own = x[s][:, :, STARTS[lv]:STARTS[lv + 1]]
                        nc.vector.scalar_tensor_tensor(own, columns(step[s], lv), b2wy[:], own,
                                                       ALU.add, ALU.add).then_inc(updated[s], 1)
                        if lv + 1 < LEVELS:
                            dve.wait_ge(updated[s], r * LEVELS + lv + 1)
                            new_neighbours(s, lv + 1, r)

        @block.scalar
        def _(act):
            act.wait_ge(weights_in, 16 * 7)
            with act.Fori(0, ROUNDS) as r:
                for lv in range(LEVELS):
                    for s in each:
                        act.wait_ge(pre_ready[s], r * LEVELS + lv + 1)
                        for h in range(HALVES):
                            nc.scalar.activation(cells(hidden[s][h], lv), columns(pre[s][lv % 2], lv, h),
                                                 ACT.Tanh, bias=b1_col[:, h:h + 1]
                                                 ).then_inc(tanh_ready[s], 1)

        @block.tensor
        def _(pe):
            pe.wait_ge(weights_ready, 2 + HALVES)

            def own_products(s, lv):
                for h in range(HALVES):
                    mm = nc.tensor.matmul(columns(pre[s][lv % 2], lv, h), w1_own[:, h * P:(h + 1) * P],
                                          x[s][:, :, STARTS[lv]:STARTS[lv + 1]],
                                          start=(h == 0), stop=False, skip_group_check=True)

            def near_products(s, lv, r):
                pe.wait_ge(near_ready[s], r * LEVELS + lv + 1)
                for h in range(HALVES):
                    mm = nc.tensor.matmul(columns(pre[s][lv % 2], lv, h), w1_sum[:, h * P:(h + 1) * P],
                                          cells(near[s][lv % 2], lv),
                                          start=False, stop=(h == HALVES - 1), skip_group_check=True)
                mm.then_inc(pre_ready[s], 1)

            def step_products(s, lv, r):
                for h in range(HALVES):
                    pe.wait_ge(tanh_ready[s], (r * LEVELS + lv) * HALVES + h + 1)
                    mm = nc.tensor.matmul(columns(step[s], lv), w2wy[h][:], cells(hidden[s][h], lv),
                                          start=(h == 0), stop=(h == HALVES - 1))
                mm.then_inc(step_ready[s], 1)

            with pe.Fori(0, ROUNDS) as r:
                for k in range(NC):
                    pe.wait_ge(loaded[k], 16 * STREAMS * (r + 1))
                for s in each:
                    own_products(s, 0)
                for lv in range(LEVELS):
                    near_products(0, lv, r)
                    if lv > 0:
                        step_products(1, lv - 1, r)
                        own_products(1, lv)
                    near_products(1, lv, r)
                    step_products(0, lv, r)
                    if lv + 1 < LEVELS:
                        own_products(0, lv + 1)
                step_products(1, LEVELS - 1, r)



def attention_layer(nc, sems, tag, psum, src, dst, wq, bq, wk, bk, wv, bv, gamma):
    MT = CELLS // P
    HALVES = CELLS // BANK
    DEEP = 4
    PROBS = 4
    LOW_ROW, HIGH_ROW = 80, 96

    with ExitStack() as ctx:
        sb = lambda name, shape, dt=F32: ctx.enter_context(nc.sbuf_tensor(f"{tag}_{name}", shape, dt))
        sem = lambda name: sems.enter_context(nc.semaphore(f"{tag}_{name}"))

        x = [sb(f"x{u}", [P, CELLS]) for u in range(DEEP)]
        q = [sb(f"q{u}", [P, CELLS], F32R) for u in range(DEEP)]
        k = [sb(f"k{u}", [P, CELLS], F32R) for u in range(DEEP)]
        v = [sb(f"v{u}", [P, MT, P]) for u in range(DEEP)]
        probs = [sb(f"probs{n}", [P, CELLS]) for n in range(PROBS)]
        psum_keys = [sb(f"prob_sum{u}", [P, CELLS]) for u in range(2)]
        mixed = [sb(f"mixed{u}", [P, CELLS]) for u in range(2)]
        scaled = sb("scaled", [P, CELLS])
        out = [sb(f"out{u}", [P, CELLS]) for u in range(2)]
        top = [sb(f"top{u}", [P, MT]) for u in range(2)]
        minus_top = [sb(f"minus_top{u}", [P, MT, P], F32R) for u in range(2)]
        share = sb("share", [P, MT])
        wq_rows = sb("wq_rows", [P, P])
        wk_rows = sb("wk_rows", [P, P])
        wv_sb = sb("wv_sb", [P, P])
        bq_rows = sb("bq_rows", [P, 1])
        bk_rows = sb("bk_rows", [P, 1])
        bv_col = sb("bv_col", [P, 1])
        gamma_col = sb("gamma_col", [P, 1])
        ident = sb("ident", [P, P])
        ident_r = sb("ident_r", [P, P], F32R)
        ones = sb("ones", [P, 1])

        rows_ps, keys_ps, mix_ps, misc_ps = psum

        weights_in, consts_ready, ident_turn = sem("weights_in"), sem("consts_ready"), sem("ident_turn")
        x_in = [sem(f"x_in{u}") for u in range(DEEP)]
        out_stored = [sem(f"out_stored{u}") for u in range(2)]
        k_proj, q_proj, v_proj = sem("k_proj"), sem("q_proj"), sem("v_proj")
        k_high, q_high, v_ready = sem("k_high"), sem("q_high"), sem("v_ready")
        k_low, q_low = sem("k_low"), sem("q_low")
        rows_ready, row_max = sem("rows_ready"), sem("row_max")
        top_high, top_low, top_rows, top_added = (sem(n) for n in ("top_high", "top_low", "top_rows", "top_added"))
        keys_ready, probs_ready = sem("keys_ready"), sem("probs_ready")
        probs_mixed, probs_summed = sem("probs_mixed"), sem("probs_summed")
        mix_copied = sem("mix_copied")
        sum_cols, share_ready, share_rows = sem("sum_cols"), sem("share_ready"), sem("share_rows")
        share_turn, scaled_ready, out_ready = sem("share_turn"), sem("scaled_ready"), sem("out_ready")
        block = ctx.enter_context(nc.Block())

        WEIGHTS = 14 + (gamma is not None)
        CONSTS = 6 + (gamma is None) + 2

        def steps(part):
            def exists(i, u):
                return lambda d: not isinstance(i, int) or 0 <= DEEP * i + u + d < BATCH
            for u in (-2, -1, *range(DEEP)):
                part(0, u, exists(0, u))
            return exists

        def pipeline(engine, part):
            exists = steps(part)
            with engine.Fori(1, BATCH // DEEP - 1) as i:
                for u in range(DEEP):
                    part(i, u, exists(i, u))
            last = BATCH // DEEP - 1
            for u in range(DEEP + 1):
                part(last, u, exists(last, u))

        @block.sync
        def _(sp):
            sp.wait_ge(consts_ready, CONSTS)
            with nc.allow_non_contiguous_dma(reason="small weight columns"):
                for g in range(3):
                    rows = slice(32 * g, 32 * g + DQK)
                    sp.dma_start(wq_rows[:, rows], wq).then_inc(weights_in, 16)
                    sp.dma_start(wk_rows[:, rows], wk).then_inc(weights_in, 16)
                for g in range(3):
                    rows = slice(32 * g, 32 * g + DQK)
                    sp.dma_start(bq_rows[rows, :], bq.rearrange("(d a) -> d a", a=1)).then_inc(weights_in, 16)
                    sp.dma_start(bk_rows[rows, :], bk.rearrange("(d a) -> d a", a=1)).then_inc(weights_in, 16)
                sp.dma_start(wv_sb[:], wv).then_inc(weights_in, 16)
                sp.dma_start(bv_col[:], bv.rearrange("(c a) -> c a", a=1)).then_inc(weights_in, 16)
                if gamma is not None:
                    sp.dma_start(gamma_col[:], gamma.to_broadcast([P, 1])).then_inc(weights_in, 16)

            def part(i, u, job):
                j = DEEP * i + u
                if job(3):
                    positive(sp, out_ready, j)
                    sp.dma_start(x[(u + 3) % DEEP][:], src[bass.ds(j + 3, 1), :, :].rearrange("b c n -> c (b n)")
                                 ).then_inc(x_in[(u + 3) % DEEP], 16)
                if job(-1):
                    sp.wait_ge(out_ready, j)
                    sp.dma_start(dst[bass.ds(j - 1, 1), :, :].rearrange("b c n -> c (b n)"),
                                 out[(u - 1) % 2][:]).then_inc(out_stored[(u - 1) % 2], 16)

            sp.dma_start(x[0][:], src[0, :, :]).then_inc(x_in[0], 16)
            pipeline(sp, part)
            for u in range(2):
                sp.wait_ge(out_stored[u], 16 * BATCH // 2)

        @block.gpsimd
        def _(pool):
            nc.gpsimd.memset(wq_rows[:], 0.0).then_inc(consts_ready, 1)
            nc.gpsimd.memset(wk_rows[:], 0.0).then_inc(consts_ready, 1)
            nc.gpsimd.memset(bq_rows[:], 0.0).then_inc(consts_ready, 1)
            nc.gpsimd.memset(bk_rows[:], 0.0).then_inc(ident_turn, 1)
            nc.gpsimd.memset(ones[:], 1.0).then_inc(consts_ready, 1)
            nc.gpsimd.memset(ident[:], 0.0).then_inc(ident_turn, 1)
            pool.wait_ge(ident_turn, 2)
            nc.gpsimd.affine_select(out=bk_rows[:], in_=bk_rows[:], compare_op=ALU.not_equal, fill=1.0,
                                    base=-LOW_ROW, pattern=[[0, 1]], channel_multiplier=1).then_inc(ident_turn, 1)
            nc.gpsimd.affine_select(out=ident[:], in_=ident[:], compare_op=ALU.not_equal, fill=1.0,
                                    base=0, pattern=[[-1, P]], channel_multiplier=1).then_inc(consts_ready, 1)
            pool.wait_ge(ident_turn, 3)
            nc.gpsimd.affine_select(out=bk_rows[:], in_=bk_rows[:], compare_op=ALU.not_equal, fill=1.0,
                                    base=-HIGH_ROW, pattern=[[0, 1]], channel_multiplier=1).then_inc(consts_ready, 1)
            if gamma is None:
                nc.gpsimd.memset(gamma_col[:], 1.0).then_inc(consts_ready, 1)

            def part(i, u, job):
                if not job(0):
                    return
                j = DEEP * i + u
                total = psum_keys[u % 2]
                positive(pool, sum_cols, j - 1)
                for t in range(1, MT):
                    pool.wait_ge(probs_ready, (MT * j + t + 1) * HALVES)
                    if t > 1:
                        pool.wait_ge(probs_summed, (MT - 1) * j + t - 1)
                    in0 = probs[0][:] if t == 1 else total[:]
                    nc.gpsimd.tensor_tensor(total[:], in0, probs[t % PROBS][:], ALU.add
                                            ).then_inc(probs_summed, 1)

            pipeline(pool, part)

        @block.vector
        def _(dve):
            for u in range(2):
                nc.vector.memset(minus_top[u][:].bitcast(F32), 0.0).then_inc(consts_ready, 1)
            dve.wait_ge(consts_ready, CONSTS)
            nc.vector.tensor_copy(ident_r[:], ident[:]).then_inc(ident_turn, 1)
            dve.wait_ge(weights_in, 16 * WEIGHTS)
            nc.vector.tensor_tensor(bv_col[:], bv_col[:], gamma_col[:], ALU.mult).then_inc(ident_turn, 1)
            dve.wait_ge(ident_turn, 5)

            def part(i, u, job):
                j = DEEP * i + u
                nxt, new, old = (u + 1) % DEEP, (u + 2) % DEEP, (u - 1) % DEEP

                def row_maximum(t):
                    if job(1):
                        dve.wait_ge(rows_ready, MT * (j + 1) + t + 1)
                        nc.vector.reduce_max(top[nxt % 2][:, t:t + 1], rows_ps[:], AX_X).then_inc(row_max, 1)

                row_maximum(0)
                if job(-1):
                    dve.wait_ge(sum_cols, j)
                    positive(dve, share_rows, j - 1)
                    nc.vector.reciprocal(share[:], misc_ps[:, 0:MT]).then_inc(share_turn, 1)
                    dve.wait_ge(share_turn, j)
                    nc.vector.tensor_scalar(share[:], share[:], gamma_col[:], None, ALU.mult).then_inc(share_ready, 1)
                    dve.wait_ge(share_rows, j)
                    dve.wait_ge(mix_copied, j)
                    positive(dve, out_ready, j - 1)
                    nc.vector.tensor_tensor(scaled[:], misc_ps[:], mixed[old % 2][:], ALU.mult).then_inc(scaled_ready, 1)
                row_maximum(1)
                if job(-1):
                    dve.wait_ge(scaled_ready, j)
                    stores = 16 * ((DEEP // 2) * i + (u - 1) // 2)
                    positive(dve, out_stored[old % 2], stores)
                    nc.vector.scalar_tensor_tensor(out[old % 2][:], scaled[:], bv_col[:], x[old][:],
                                                   ALU.add, ALU.add).then_inc(out_ready, 1)
                if job(2):
                    dve.wait_ge(k_high, j + 3)
                    rows = slice(32, 64)
                    nc.vector.scalar_tensor_tensor(k[new][rows, :], misc_ps[rows, :], bk_rows[rows, :], k[new][rows, :],
                                                   ALU.add, ALU.subtract).then_inc(k_low, 1)
                row_maximum(2)
                if job(2):
                    dve.wait_ge(q_high, j + 3)
                    rows = slice(64, 96)
                    nc.vector.scalar_tensor_tensor(q[new][rows, :], misc_ps[rows, :], bq_rows[rows, :], q[new][rows, :],
                                                   ALU.add, ALU.subtract).then_inc(q_low, 1)
                for t in range(3, MT):
                    row_maximum(t)
                if job(1):
                    tops, minus = top[nxt % 2], minus_top[nxt % 2]
                    dve.wait_ge(row_max, MT * (j + 2))
                    positive(dve, top_rows, j)
                    nc.vector.tensor_scalar(minus[:, :, HIGH_ROW], tops[:], -1.0, None, ALU.mult).then_inc(top_high, 1)
                    dve.wait_ge(top_high, j + 2)
                    nc.vector.scalar_tensor_tensor(minus[:, :, LOW_ROW], tops[:], -1.0, minus[:, :, HIGH_ROW],
                                                   ALU.mult, ALU.subtract).then_inc(top_low, 1)
                    dve.wait_ge(top_rows, j + 2)
                    rows = slice(64, P)
                    nc.vector.tensor_tensor(q[nxt][rows, :], misc_ps[rows, :], q[nxt][rows, :],
                                            ALU.add).then_inc(top_added, 1)

            pipeline(dve, part)

        @block.scalar
        def _(act):
            act.wait_ge(weights_in, 16 * WEIGHTS)
            act.wait_ge(ident_turn, 5)

            def part(i, u, job):
                j = DEEP * i + u
                new = (u + 2) % DEEP

                def exponentials(t):
                    if not job(0):
                        return
                    tile = probs[t % PROBS]
                    for h in range(HALVES):
                        act.wait_ge(keys_ready, (MT * j + t) * HALVES + h + 1)
                        if h == 0:
                            positive(act, probs_mixed, MT * j + t - PROBS + 1)
                            if t >= PROBS:
                                before = (MT - 1) * j + (t - PROBS if t > PROBS else 1)
                            else:
                                before = (MT - 1) * (j - 1) + MT - PROBS + t
                            positive(act, probs_summed, before)
                        half = slice(h * BANK, (h + 1) * BANK)
                        nc.scalar.activation(tile[:, half], keys_ps[:, half], ACT.Exp).then_inc(probs_ready, 1)

                if job(-1):
                    act.wait_ge(probs_mixed, MT * j)
                    positive(act, scaled_ready, j - 2)
                    nc.scalar.activation(mixed[(u - 1) % 2][:], mix_ps[:], ACT.Copy).then_inc(mix_copied, 1)
                exponentials(0)
                exponentials(1)
                if job(2):
                    act.wait_ge(k_proj, j + 3)
                    nc.scalar.activation(k[new][:], misc_ps[:], ACT.Identity, bias=bk_rows[:]).then_inc(k_high, 1)
                exponentials(2)
                if job(2):
                    act.wait_ge(q_proj, j + 3)
                    nc.scalar.activation(q[new][:], misc_ps[:], ACT.Identity, bias=bq_rows[:]).then_inc(q_high, 1)
                exponentials(3)
                if job(2):
                    act.wait_ge(v_proj, j + 3)
                    nc.scalar.activation(v[new][:].rearrange("p t c -> p (t c)"), misc_ps[:],
                                         ACT.Copy).then_inc(v_ready, 1)
                for t in range(4, MT):
                    exponentials(t)

            pipeline(act, part)

        @block.tensor
        def _(pe):
            pe.wait_ge(weights_in, 16 * WEIGHTS)
            pe.wait_ge(ident_turn, 5)

            def part(i, u, job):
                j = DEEP * i + u
                cur, nxt, new, old = u % DEEP, (u + 1) % DEEP, (u + 2) % DEEP, (u - 1) % DEEP

                def key_energies(t):
                    if not job(0):
                        return
                    if t == 0:
                        pe.wait_ge(top_added, j + 1)
                    for h in range(HALVES):
                        half = slice(h * BANK, (h + 1) * BANK)
                        positive(pe, probs_ready, (MT * j + t - 1) * HALVES + h + 1)
                        nc.tensor.matmul(keys_ps[:, half], k[cur][:, t * P:(t + 1) * P], q[cur][:, half],
                                         start=True, stop=True).then_inc(keys_ready, 1)

                def row_energies(t):
                    if not job(1):
                        return
                    if t == 0:
                        pe.wait_ge(k_low, j + 2)
                        pe.wait_ge(q_low, j + 2)
                    positive(pe, row_max, MT * (j + 1) + t)
                    for h in range(HALVES):
                        half = slice(h * BANK, (h + 1) * BANK)
                        mm = nc.tensor.matmul(rows_ps[:, half], q[nxt][:, t * P:(t + 1) * P], k[nxt][:, half],
                                              start=True, stop=True)
                    mm.then_inc(rows_ready, 1)

                def mix(t, h):
                    if not job(0):
                        return
                    if t == 0 and h == 0:
                        pe.wait_ge(v_ready, j + 1)
                        positive(pe, mix_copied, j)
                    half = slice(h * BANK, (h + 1) * BANK)
                    pe.wait_ge(probs_ready, (MT * j + t) * HALVES + h + 1)
                    mm = nc.tensor.matmul(mix_ps[:, half], v[cur][:, t, :], probs[t % PROBS][:, half],
                                          start=(t == 0), stop=(t == MT - 1))
                    if h == HALVES - 1:
                        mm.then_inc(probs_mixed, 1)

                def project(weights, done):
                    for h in range(HALVES):
                        half = slice(h * BANK, (h + 1) * BANK)
                        mm = nc.tensor.matmul(misc_ps[:, half], weights[:], x[new][:, half], start=True, stop=True)
                    mm.then_inc(done, 1)

                key_energies(0)
                row_energies(0)
                if job(-1):
                    pe.wait_ge(probs_summed, (MT - 1) * j)
                    if job(0):
                        pe.wait_ge(top_added, j + 1)
                    positive(pe, scaled_ready, j - 1)
                    for t in range(MT):
                        mm = nc.tensor.matmul(misc_ps[:, t:t + 1], psum_keys[old % 2][:, t * P:(t + 1) * P], ones[:],
                                              start=True, stop=True)
                    mm.then_inc(sum_cols, 1)
                key_energies(1)
                if job(-1):
                    pe.wait_ge(share_ready, j)
                    for t in range(MT):
                        mm = nc.tensor.matmul(misc_ps[:, t * P:(t + 1) * P], share[:, t:t + 1].to_broadcast([P, P]),
                                              ident[:], start=True, stop=True)
                    mm.then_inc(share_rows, 1)
                row_energies(1)
                mix(0, 0)
                mix(0, 1)
                key_energies(2)
                if job(2):
                    pe.wait_ge(x_in[new], 16 * i + 16 * ((u + 2) // DEEP + 1))
                    positive(pe, v_ready, j + 2)
                    positive(pe, scaled_ready, j)
                    positive(pe, top_added, j + 1)
                    project(wk_rows, k_proj)
                row_energies(2)
                mix(1, 0)
                mix(1, 1)
                key_energies(3)
                if job(2):
                    pe.wait_ge(k_low, j + 3)
                    project(wq_rows, q_proj)
                row_energies(3)
                mix(2, 0)
                mix(2, 1)
                key_energies(4)
                if job(2):
                    pe.wait_ge(q_low, j + 3)
                    for t in range(MT):
                        mm = nc.tensor.matmul(misc_ps[:, t * P:(t + 1) * P], x[new][:, t * P:(t + 1) * P], wv_sb[:],
                                              start=True, stop=True)
                    mm.then_inc(v_proj, 1)
                row_energies(4)
                mix(3, 0)
                mix(3, 1)
                for t in range(5, MT):
                    key_energies(t)
                    row_energies(t)
                    mix(t - 1, 0)
                    mix(t - 1, 1)
                mix(MT - 1, 0)
                if job(1):
                    pe.wait_ge(top_low, j + 2)
                    pe.wait_ge(v_ready, j + 3) if job(2) else None
                    for t in range(MT):
                        mm = nc.tensor.matmul(misc_ps[:, t * P:(t + 1) * P], minus_top[nxt % 2][:, t, :], ident_r[:],
                                              start=True, stop=True)
                    mm.then_inc(top_rows, 1)
                mix(MT - 1, 1)

            pipeline(pe, part)


def build(nc, t):
    with ExitStack() as ctx:
        psum = [ctx.enter_context(nc.psum_tensor(f"psum{n}", [P, CELLS], F32)) for n in range(4)]
        layers(nc, ctx, psum, t)


def layers(nc, sems, psum, t):
    inner = [nc.dram_tensor(f"layer{n}_out", [BATCH, P, CELLS], F32, kind="Internal").ap() for n in range(3)]
    scan_layer(nc, sems, "L0", psum, t["x_cells"], inner[0], *(t[f"L0_conv_{n}"] for n in ("w1", "b1", "w2", "b2", "w_y")))
    attention_layer(nc, sems, "L1", psum, inner[0], inner[1],
                    *(t[f"L1_conv_{n}"] for n in ("Wq", "bq", "Wk", "bk", "Wv", "bv", "gamma")))
    attention_layer(nc, sems, "L2", psum, inner[1], inner[2],
                    *(t[f"L2_conv_{n}"] for n in ("wq", "bq", "wk", "bk", "wv", "bv")), None)
    scan_layer(nc, sems, "L3", psum, inner[2], t["y_cells"], *(t[f"L3_conv_{n}"] for n in ("w1", "b1", "w2", "b2", "w_y")))


def kernel(**inputs):
    import concourse.bacc as bacc
    from concourse.bass_utils import run_bass_kernel_spmd

    arrays = {n: np.asarray(a) for n, a in inputs.items()}
    x = arrays.pop("x").reshape(BATCH, CELLS, P)[:, GRID, :]
    arrays["x_cells"] = np.ascontiguousarray(x.transpose(0, 2, 1))
    for n in ("L0_conv_b2", "L3_conv_b2", "L1_conv_gamma"):
        arrays[n] = arrays[n].reshape(1, 1)
    nc = bacc.Bacc("TRN2", target_bir_lowering=False, num_devices=1)
    t = {n: nc.dram_tensor(n, a.shape, F32, kind="ExternalInput").ap() for n, a in arrays.items()}
    t["y_cells"] = nc.dram_tensor("y_cells", [BATCH, P, CELLS], F32, kind="ExternalOutput").ap()
    build(nc, t)
    got = run_bass_kernel_spmd(nc, [arrays], core_ids=[0]).results[0]["y_cells"]
    y = np.empty((BATCH, CELLS, P), np.float32)
    y[:, GRID, :] = got.transpose(0, 2, 1)
    return y.reshape(BATCH, SIDE, SIDE, P)
```

```python
from contextlib import ExitStack

import numpy as np

import concourse.bass as bass
from concourse import mybir

F32 = mybir.dt.float32
F32R = mybir.dt.float32r
ALU = mybir.AluOpType
ACT = mybir.ActivationFunctionType
AX_X = mybir.AxisListType.X

P = 128
SIDE = 32
CELLS = SIDE * SIDE
BATCH = 64
HID = 256
DQK = 16
BANK = 512



def spiral_path():
    cy = cx = SIDE // 2
    path, seen = [], set()

    def visit(ring, y, x):
        if 0 <= y < SIDE and 0 <= x < SIDE and (y, x) not in seen:
            seen.add((y, x))
            path.append((ring, y, x))

    visit(0, cy, cx)
    for r in range(1, SIDE // 2 + 1):
        top, bottom, left, right = cy - r, cy + r, cx - r, cx + r
        for x in range(left, right + 1):
            visit(r, top, x)
        for y in range(top + 1, bottom + 1):
            visit(r, y, right)
        for x in range(right - 1, left - 1, -1):
            visit(r, bottom, x)
        for y in range(bottom - 1, top, -1):
            visit(r, y, left)
    return path


LATE, OLD, NEW, STEP = range(4)


def neighbours(y, x):
    near = ((y - 1, x), (y + 1, x), (y, x - 1), (y, x + 1))
    return [(a, b) for a, b in near if 0 <= a < SIDE and 0 <= b < SIDE]


def wavefront():
    path = spiral_path()
    rank = {(y, x): n for n, (_, y, x) in enumerate(path)}
    level, ring = {}, {}
    for n, (r, y, x) in enumerate(path):
        earlier = [level[c] for c in neighbours(y, x) if rank[c] < n]
        level[y, x] = max(earlier, default=-1 if (y, x) != (0, 0) else 0) + 1
        ring[y, x] = r
    order = sorted(level, key=lambda c: (level[c], ring[c]))
    at = {c: n for n, c in enumerate(order)}
    starts = [0]
    for n, c in enumerate(order):
        if level[c] == len(starts):
            starts.append(n)
    starts.append(CELLS)

    sums_late, sums_old, sums_new, steps, edges, last_read = [], [], [], [], [], [0] * CELLS
    for lv in range(len(starts) - 1):
        late_ops, old_ops, new_ops, step_ops, edge_runs = [], [], [], [], []

        def run(ops, key, n, a, b):
            if ops and ops[-1][0] == key:
                _, n0, k, a0, b0 = ops[-1]
                follows = all((s is None) == (s0 is None) and (s is None or s == s0 + k)
                              for s, s0 in ((a, a0), (b, b0)))
                if n == n0 + k and follows:
                    ops[-1] = (key, n0, k + 1, a0, b0)
                    return
            ops.append((key, n, 1, a, b))

        by_turn = {}
        ops = {LATE: late_ops, OLD: old_ops, NEW: new_ops}
        for n in range(starts[lv], starts[lv + 1]):
            c = order[n]
            near = neighbours(*c)
            late = sorted((at[d] for d in near if rank[d] > rank[c]), reverse=True)
            early = sorted(at[d] for d in near if rank[d] < rank[c])
            before = [a for a in early if rank[order[a]] == rank[c] - 1]
            early = [a for a in early if a not in before]
            assert all(level[order[a]] < lv for a in early + before)
            assert all(level[order[a]] > lv for a in late)
            for a in early + before:
                last_read[a] = max(last_read[a], lv)
            old = [a for a in early if level[order[a]] < lv - 1]
            new = [a for a in early if level[order[a]] == lv - 1] + before
            terms = ([(a, LATE, t) for t, a in enumerate(late)] + [(a, OLD, t) for t, a in enumerate(old)]
                     + [(a, NEW, t) for t, a in enumerate(new, 4 - len(new))])
            (a, kind, _), (b, kind_b, t) = terms[:2]
            assert kind != NEW
            by_turn.setdefault((kind_b, t), []).append((n, a, b))
            for a, kind, t in terms[2:]:
                by_turn.setdefault((kind, t), []).append((n, None, a))
            if len(near) < 4:
                run(edge_runs, len(near), n, None, None)
            for t, a in enumerate(new, 4 - len(new)):
                by_turn.setdefault((STEP, t), []).append((n, 4 / len(near), a))
        for (kind, turn), terms in sorted(by_turn.items()):
            for n, a, b in terms:
                if kind == STEP:
                    run(step_ops, (turn, a), n, None, b)
                else:
                    run(ops[kind], turn, n, a, b)
        sums_late.append([o[1:] for o in late_ops])
        sums_old.append([o[1:] for o in old_ops])
        sums_new.append([o[1:] for o in new_ops])
        steps.append([(n, k, b, factor) for (_, factor), n, k, _, b in step_ops])
        edges.append([(n, k, count) for count, n, k, _, _ in edge_runs])
    grid = np.array([y * SIDE + x for y, x in order])
    return grid, starts, sums_late, sums_old, sums_new, steps, edges, last_read


GRID, STARTS, SUMS_LATE, SUMS_OLD, SUMS_NEW, STEPS, EDGES, LAST_READ = wavefront()
LEVELS = len(STARTS) - 1


def chunk_levels():
    first = [0, 2]
    for lv in range(2, LEVELS):
        if STARTS[lv + 1] - STARTS[first[-1]] > CELLS // 8 and lv > first[-1]:
            first.append(lv)
    return first + [LEVELS]


CHUNKS = chunk_levels()


def positive(engine, semaphore, value):
    if not isinstance(value, int) or value > 0:
        engine.wait_ge(semaphore, value)



def scan_layer(nc, sems, tag, psum, src, dst, w1, b1, w2, b2, w_y):
    IMAGES = 32
    ROUNDS = BATCH // IMAGES
    HALVES = HID // P
    WIDE = max(b - a for a, b in zip(STARTS, STARTS[1:]))
    assert WIDE * IMAGES <= BANK
    NC = len(CHUNKS) - 1

    with ExitStack() as ctx:
        sb = lambda name, shape, dt=F32: ctx.enter_context(nc.sbuf_tensor(f"{tag}_{name}", shape, dt))
        sem = lambda name: sems.enter_context(nc.semaphore(f"{tag}_{name}"))

        x = sb("x", [P, IMAGES, CELLS])
        near = [sb(f"near{k}", [P, IMAGES, WIDE]) for k in range(2)]
        hidden = [sb(f"hidden{h}", [P, IMAGES, WIDE]) for h in range(HALVES)]
        w1_own = sb("w1_own", [P, HID])
        w1_near = sb("w1_near", [P, HID])
        w1_sum = sb("w1_sum", [P, HID])
        b1_col = sb("b1_col", [P, HALVES])
        w2_col = sb("w2_col", [P, HALVES])
        wy_rows = sb("wy_rows", [P, P])
        wy_col = sb("wy_col", [P, 1])
        b2_col = sb("b2_col", [P, 1])
        b2wy = sb("b2wy", [P, 1])
        w2wy = [sb(f"w2wy{h}", [P, P]) for h in range(HALVES)]
        pre = [[psum[k][:, h * BANK:(h + 1) * BANK] for h in range(HALVES)] for k in range(2)]
        step = [psum[2][:, k * BANK:(k + 1) * BANK] for k in range(2)]

        weights_in = sem("weights_in")
        weights_ready = sem("weights_ready")
        loaded = [sem(f"loaded{k}") for k in range(NC)]
        stored = [sem(f"stored{k}") for k in range(NC)]
        late_ready = sem("late_ready")
        near_turn = sem("near_turn")
        pre_ready = sem("pre_ready")
        tanh_ready = sem("tanh_ready")
        step_ready = sem("step_ready")
        updated = sem("updated")
        block = ctx.enter_context(nc.Block())

        def images(r):
            return slice(r * IMAGES, (r + 1) * IMAGES)

        def chunk(k):
            return slice(STARTS[CHUNKS[k]], STARTS[CHUNKS[k + 1]])

        def cells(t, lv):
            return t[:, :, 0:STARTS[lv + 1] - STARTS[lv]]

        def columns(t, lv, a=None, k=None):
            n = STARTS[lv + 1] - STARTS[lv]
            a, k = (0, n) if a is None else (a - STARTS[lv], k)
            return t[:, 0:IMAGES * n].rearrange("p (b n) -> p b n", b=IMAGES)[:, :, a:a + k]

        def late_count(lv):
            return sum(len(SUMS_LATE[v]) for v in range(lv))

        def turn_count(lv):
            return sum(len(kind[v]) for kind in (SUMS_OLD, SUMS_NEW, EDGES, STEPS) for v in range(lv))

        LATE_ROUND, TURN_ROUND = late_count(LEVELS), turn_count(LEVELS)
        assert turn_count(1) == 0

        def load(sp, r, k):
            sp.dma_start(x[:, :, chunk(k)], src[images(r), :, chunk(k)].rearrange("b c n -> c b n")
                         ).then_inc(loaded[k], 16)

        def reload(sp, r, k):
            sp.wait_ge(stored[k], 16 * (r + 1))
            sp.wait_ge(updated, r * LEVELS + max(max(LAST_READ[chunk(k)]) + 1, CHUNKS[k + 1]))
            load(sp, r + 1, k)

        @block.sync
        def _(sp):
            with nc.allow_non_contiguous_dma(reason="small weight columns"):
                for dram, tile in ((w1[0:P, :], w1_own[:]), (w1[P:2 * P, :], w1_near[:]),
                                   (b1.rearrange("(h p) -> p h", p=P), b1_col[:]),
                                   (w2.rearrange("(h p) -> p h", p=P), w2_col[:]),
                                   (w_y.rearrange("(a c) -> a c", a=1).to_broadcast([P, P]), wy_rows[:]),
                                   (w_y.rearrange("(c a) -> c a", a=1), wy_col[:]),
                                   (b2.to_broadcast([P, 1]), b2_col[:])):
                    sp.dma_start(tile, dram).then_inc(weights_in, 16)
                for k in range(NC):
                    load(sp, 0, k)
                for r in range(ROUNDS):
                    for k in range(NC):
                        sp.wait_ge(updated, r * LEVELS + CHUNKS[k + 1])
                        sp.dma_start(dst[images(r), :, chunk(k)].rearrange("b c n -> c b n"),
                                     x[:, :, chunk(k)]).then_inc(stored[k], 16)
                        if r + 1 < ROUNDS and k >= 2:
                            reload(sp, r, k - 1)
                    if r + 1 < ROUNDS:
                        reload(sp, r, NC - 1)
                        reload(sp, r, 0)
                for k in range(NC):
                    sp.wait_ge(stored[k], 16 * ROUNDS)

        @block.gpsimd
        def _(pool):
            with pool.Fori(0, ROUNDS) as r:
                for k in range(NC):
                    pool.wait_ge(loaded[k], 16 * (r + 1))
                for lv in range(LEVELS):
                    if lv >= 2:
                        pool.wait_ge(pre_ready, (r * LEVELS + lv - 1) * HALVES)
                    for n, (a, k, s0, s1) in enumerate(SUMS_LATE[lv]):
                        out = near[lv % 2][:, :, a - STARTS[lv]:a - STARTS[lv] + k]
                        if s0 is None:
                            pool.wait_ge(late_ready, r * LATE_ROUND + late_count(lv) + n)
                        in0 = out if s0 is None else x[:, :, s0:s0 + k]
                        nc.gpsimd.tensor_tensor(out, in0, x[:, :, s1:s1 + k], ALU.add).then_inc(late_ready, 1)

        @block.vector
        def _(dve):
            dve.wait_ge(weights_in, 16 * 7)
            nc.vector.tensor_scalar(w1_sum[:], w1_near[:], 0.25, None, ALU.mult).then_inc(weights_ready, 1)
            nc.vector.tensor_tensor(b2wy[:], b2_col[:], wy_col[:], ALU.mult).then_inc(weights_ready, 1)
            for h in range(HALVES):
                nc.vector.tensor_scalar(w2wy[h][:], wy_rows[:], w2_col[:, h:h + 1], None,
                                        ALU.mult).then_inc(weights_ready, 1)
            dve.wait_ge(weights_ready, 2 + HALVES)

            def sum_before_step(lv, r):
                dve.wait_ge(late_ready, r * LATE_ROUND + late_count(lv + 1))
                turn = r * TURN_ROUND + turn_count(lv)
                if SUMS_OLD[lv]:
                    dve.wait_ge(updated, r * LEVELS + lv - 1)
                n = 0
                for op in (*SUMS_OLD[lv], *SUMS_NEW[lv]):
                    a, k, s0, s1 = op
                    out = near[lv % 2][:, :, a - STARTS[lv]:a - STARTS[lv] + k]
                    if s0 is None and n > 0:
                        dve.wait_ge(near_turn, turn + n)
                    in0 = out if s0 is None else x[:, :, s0:s0 + k]
                    if n < len(SUMS_OLD[lv]):
                        nc.vector.tensor_tensor(out, in0, x[:, :, s1:s1 + k], ALU.add).then_inc(near_turn, 1)
                    else:
                        nc.vector.scalar_tensor_tensor(out, x[:, :, s1:s1 + k], b2wy[:], in0,
                                                       ALU.add, ALU.add).then_inc(near_turn, 1)
                    n += 1
                for a, k, count in EDGES[lv]:
                    out = near[lv % 2][:, :, a - STARTS[lv]:a - STARTS[lv] + k]
                    if n > 0:
                        dve.wait_ge(near_turn, turn + n)
                    nc.vector.tensor_scalar(out, out, 4.0 / count, None, ALU.mult).then_inc(near_turn, 1)
                    n += 1
                return turn, n

            def add_steps(lv, turn, n):
                dve.wait_ge(near_turn, turn + n)
                written = set()
                for a, k, s1, factor in STEPS[lv]:
                    if written & set(range(a, a + k)):
                        dve.wait_ge(near_turn, turn + n)
                    written |= set(range(a, a + k))
                    out = near[lv % 2][:, :, a - STARTS[lv]:a - STARTS[lv] + k]
                    nc.vector.scalar_tensor_tensor(out, columns(step[(lv - 1) % 2], lv - 1, s1, k), factor, out,
                                                   ALU.mult, ALU.add).then_inc(near_turn, 1)
                    n += 1

            with dve.Fori(0, ROUNDS) as r:
                for lv in range(LEVELS):
                    if lv + 1 < LEVELS:
                        done = sum_before_step(lv + 1, r)
                    dve.wait_ge(step_ready, r * LEVELS + lv + 1)
                    if lv + 1 < LEVELS:
                        add_steps(lv + 1, *done)
                    own = x[:, :, STARTS[lv]:STARTS[lv + 1]]
                    nc.vector.scalar_tensor_tensor(own, columns(step[lv % 2], lv), b2wy[:], own,
                                                   ALU.add, ALU.add).then_inc(updated, 1)

        @block.scalar
        def _(act):
            act.wait_ge(weights_in, 16 * 7)
            with act.Fori(0, ROUNDS) as r:
                for lv in range(LEVELS):
                    for h in range(HALVES):
                        act.wait_ge(pre_ready, (r * LEVELS + lv) * HALVES + h + 1)
                        nc.scalar.activation(cells(hidden[h], lv), columns(pre[lv % 2][h], lv),
                                             ACT.Tanh, bias=b1_col[:, h:h + 1]).then_inc(tanh_ready, 1)

        @block.tensor
        def _(pe):
            pe.wait_ge(weights_ready, 2 + HALVES)

            def own_products(lv):
                for h in range(HALVES):
                    nc.tensor.matmul(columns(pre[lv % 2][h], lv), w1_own[:, h * P:(h + 1) * P],
                                     x[:, :, STARTS[lv]:STARTS[lv + 1]], start=True, stop=False)

            with pe.Fori(0, ROUNDS) as r:
                for k in range(NC):
                    pe.wait_ge(loaded[k], 16 * (r + 1))
                own_products(0)
                for lv in range(LEVELS):
                    if lv == 0:
                        pe.wait_ge(late_ready, r * LATE_ROUND + late_count(1))
                    else:
                        pe.wait_ge(near_turn, r * TURN_ROUND + turn_count(lv + 1))
                    for h in range(HALVES):
                        nc.tensor.matmul(columns(pre[lv % 2][h], lv), w1_sum[:, h * P:(h + 1) * P],
                                         cells(near[lv % 2], lv), start=False, stop=True).then_inc(pre_ready, 1)
                    for h in range(HALVES):
                        pe.wait_ge(tanh_ready, (r * LEVELS + lv) * HALVES + h + 1)
                        mm = nc.tensor.matmul(columns(step[lv % 2], lv), w2wy[h][:], cells(hidden[h], lv),
                                              start=(h == 0), stop=(h == HALVES - 1))
                    mm.then_inc(step_ready, 1)
                    if lv + 1 < LEVELS:
                        own_products(lv + 1)



def attention_layer(nc, sems, tag, psum, src, dst, wq, bq, wk, bk, wv, bv, gamma):
    MT = CELLS // P
    HALVES = CELLS // BANK
    DEEP = 4
    PROBS = 4
    SHARES = 4
    LOW_ROW, HIGH_ROW = 80, 96

    with ExitStack() as ctx:
        sb = lambda name, shape, dt=F32: ctx.enter_context(nc.sbuf_tensor(f"{tag}_{name}", shape, dt))
        sem = lambda name: sems.enter_context(nc.semaphore(f"{tag}_{name}"))

        x = [sb(f"x{u}", [P, CELLS]) for u in range(DEEP)]
        q = [sb(f"q{u}", [P, CELLS], F32R) for u in range(DEEP)]
        k = [sb(f"k{u}", [P, CELLS], F32R) for u in range(DEEP)]
        v = [sb(f"v{u}", [P, MT, P]) for u in range(DEEP)]
        probs = [sb(f"probs{n}", [P, CELLS]) for n in range(PROBS)]
        psum_keys = [sb(f"prob_sum{u}", [P, CELLS]) for u in range(2)]
        mixed = [sb(f"mixed{u}", [P, CELLS]) for u in range(2)]
        scaled = sb("scaled", [P, CELLS])
        out = [sb(f"out{u}", [P, CELLS]) for u in range(2)]
        top = [sb(f"top{u}", [P, MT]) for u in range(2)]
        minus_top = [sb(f"minus_top{u}", [P, MT, P], F32R) for u in range(2)]
        share = sb("share", [P, CELLS])
        wq_rows = sb("wq_rows", [P, P])
        wk_rows = sb("wk_rows", [P, P])
        wv_sb = sb("wv_sb", [P, P])
        bq_rows = sb("bq_rows", [P, 1])
        bk_rows = sb("bk_rows", [P, 1])
        bv_col = sb("bv_col", [P, 1])
        gamma_col = sb("gamma_col", [P, 1])
        ident = sb("ident", [P, P])
        ident_r = sb("ident_r", [P, P], F32R)
        ones = sb("ones", [P, P])

        rows_ps, keys_ps, mix_ps, misc_ps = psum

        weights_in, consts_ready, ident_turn = sem("weights_in"), sem("consts_ready"), sem("ident_turn")
        x_in = [sem(f"x_in{u}") for u in range(DEEP)]
        out_stored = [sem(f"out_stored{u}") for u in range(2)]
        k_proj, q_proj, v_proj = sem("k_proj"), sem("q_proj"), sem("v_proj")
        k_high, q_high, v_ready = sem("k_high"), sem("q_high"), sem("v_ready")
        k_low, q_low = sem("k_low"), sem("q_low")
        rows_ready, row_max = sem("rows_ready"), sem("row_max")
        top_high, top_low, top_rows, top_added = (sem(n) for n in ("top_high", "top_low", "top_rows", "top_added"))
        keys_ready, probs_ready = sem("keys_ready"), sem("probs_ready")
        probs_mixed, probs_summed = sem("probs_mixed"), sem("probs_summed")
        mix_copied = sem("mix_copied")
        sum_rows, sum_copied = sem("sum_rows"), sem("sum_copied")
        share_ready = sem("share_ready")
        scaled_ready, out_ready = sem("scaled_ready"), sem("out_ready")
        block = ctx.enter_context(nc.Block())

        WEIGHTS = 14 + (gamma is not None)
        CONSTS = 6 + (gamma is None) + 2

        def steps(part):
            def exists(i, u):
                return lambda d: not isinstance(i, int) or 0 <= DEEP * i + u + d < BATCH
            for u in (-2, -1, *range(DEEP)):
                part(0, u, exists(0, u))
            return exists

        def pipeline(engine, part):
            exists = steps(part)
            with engine.Fori(1, BATCH // DEEP - 1) as i:
                for u in range(DEEP):
                    part(i, u, exists(i, u))
            last = BATCH // DEEP - 1
            for u in range(DEEP + 1):
                part(last, u, exists(last, u))

        @block.sync
        def _(sp):
            sp.wait_ge(consts_ready, CONSTS)
            with nc.allow_non_contiguous_dma(reason="small weight columns"):
                for g in range(3):
                    rows = slice(32 * g, 32 * g + DQK)
                    sp.dma_start(wq_rows[:, rows], wq).then_inc(weights_in, 16)
                    sp.dma_start(wk_rows[:, rows], wk).then_inc(weights_in, 16)
                for g in range(3):
                    rows = slice(32 * g, 32 * g + DQK)
                    sp.dma_start(bq_rows[rows, :], bq.rearrange("(d a) -> d a", a=1)).then_inc(weights_in, 16)
                    sp.dma_start(bk_rows[rows, :], bk.rearrange("(d a) -> d a", a=1)).then_inc(weights_in, 16)
                sp.dma_start(wv_sb[:], wv).then_inc(weights_in, 16)
                sp.dma_start(bv_col[:], bv.rearrange("(c a) -> c a", a=1)).then_inc(weights_in, 16)
                if gamma is not None:
                    sp.dma_start(gamma_col[:], gamma.to_broadcast([P, 1])).then_inc(weights_in, 16)

            def part(i, u, job):
                j = DEEP * i + u
                if job(3):
                    positive(sp, out_ready, j)
                    sp.dma_start(x[(u + 3) % DEEP][:], src[bass.ds(j + 3, 1), :, :].rearrange("b c n -> c (b n)")
                                 ).then_inc(x_in[(u + 3) % DEEP], 16)
                if job(-1):
                    sp.wait_ge(out_ready, j)
                    sp.dma_start(dst[bass.ds(j - 1, 1), :, :].rearrange("b c n -> c (b n)"),
                                 out[(u - 1) % 2][:]).then_inc(out_stored[(u - 1) % 2], 16)

            sp.dma_start(x[0][:], src[0, :, :]).then_inc(x_in[0], 16)
            pipeline(sp, part)
            for u in range(2):
                sp.wait_ge(out_stored[u], 16 * BATCH // 2)

        @block.gpsimd
        def _(pool):
            nc.gpsimd.memset(wq_rows[:], 0.0).then_inc(consts_ready, 1)
            nc.gpsimd.memset(wk_rows[:], 0.0).then_inc(consts_ready, 1)
            nc.gpsimd.memset(bq_rows[:], 0.0).then_inc(consts_ready, 1)
            nc.gpsimd.memset(bk_rows[:], 0.0).then_inc(ident_turn, 1)
            nc.gpsimd.memset(ones[:], 1.0).then_inc(consts_ready, 1)
            nc.gpsimd.memset(ident[:], 0.0).then_inc(ident_turn, 1)
            pool.wait_ge(ident_turn, 2)
            nc.gpsimd.affine_select(out=bk_rows[:], in_=bk_rows[:], compare_op=ALU.not_equal, fill=1.0,
                                    base=-LOW_ROW, pattern=[[0, 1]], channel_multiplier=1).then_inc(ident_turn, 1)
            nc.gpsimd.affine_select(out=ident[:], in_=ident[:], compare_op=ALU.not_equal, fill=1.0,
                                    base=0, pattern=[[-1, P]], channel_multiplier=1).then_inc(consts_ready, 1)
            pool.wait_ge(ident_turn, 3)
            nc.gpsimd.affine_select(out=bk_rows[:], in_=bk_rows[:], compare_op=ALU.not_equal, fill=1.0,
                                    base=-HIGH_ROW, pattern=[[0, 1]], channel_multiplier=1).then_inc(consts_ready, 1)
            if gamma is None:
                nc.gpsimd.memset(gamma_col[:], 1.0).then_inc(consts_ready, 1)

            def part(i, u, job):
                if not job(0):
                    return
                j = DEEP * i + u
                total = psum_keys[u % 2]
                positive(pool, sum_rows, j - 1)
                for t in range(1, MT):
                    pool.wait_ge(probs_ready, (MT * j + t + 1) * HALVES)
                    if t > 1:
                        pool.wait_ge(probs_summed, (MT - 1) * j + t - 1)
                    in0 = probs[0][:] if t == 1 else total[:]
                    nc.gpsimd.tensor_tensor(total[:], in0, probs[t % PROBS][:], ALU.add
                                            ).then_inc(probs_summed, 1)

            pipeline(pool, part)

        @block.vector
        def _(dve):
            for u in range(2):
                nc.vector.memset(minus_top[u][:].bitcast(F32), 0.0).then_inc(consts_ready, 1)
            dve.wait_ge(consts_ready, CONSTS)
            nc.vector.tensor_copy(ident_r[:], ident[:]).then_inc(ident_turn, 1)
            dve.wait_ge(weights_in, 16 * WEIGHTS)
            nc.vector.tensor_tensor(bv_col[:], bv_col[:], gamma_col[:], ALU.mult).then_inc(ident_turn, 1)
            nc.vector.tensor_scalar(wv_sb[:], wv_sb[:], gamma_col[:], None, ALU.mult).then_inc(ident_turn, 1)
            dve.wait_ge(ident_turn, 6)

            def part(i, u, job):
                j = DEEP * i + u
                nxt, new, old = (u + 1) % DEEP, (u + 2) % DEEP, (u - 1) % DEEP

                def row_maximum(t):
                    if job(1):
                        dve.wait_ge(rows_ready, MT * (j + 1) + t + 1)
                        nc.vector.reduce_max(top[nxt % 2][:, t:t + 1], rows_ps[:], AX_X).then_inc(row_max, 1)

                def invert_sums(part_of):
                    if job(-1):
                        dve.wait_ge(sum_copied, j)
                        cols = slice(part_of * CELLS // SHARES, (part_of + 1) * CELLS // SHARES)
                        nc.vector.reciprocal(share[:, cols], share[:, cols]).then_inc(share_ready, 1)

                def low_part(to, rows, bias, high, done):
                    if job(2):
                        dve.wait_ge(high, j + 3)
                        nc.vector.scalar_tensor_tensor(to[new][rows, :], misc_ps[rows, :], bias[rows, :],
                                                       to[new][rows, :], ALU.add, ALU.subtract).then_inc(done, 1)

                row_maximum(0)
                row_maximum(1)
                invert_sums(0)
                row_maximum(2)
                low_part(k, slice(32, 64), bk_rows, k_high, k_low)
                invert_sums(1)
                row_maximum(3)
                low_part(q, slice(64, 96), bq_rows, q_high, q_low)
                row_maximum(4)
                invert_sums(2)
                row_maximum(5)
                invert_sums(3)
                row_maximum(6)
                if job(-1):
                    dve.wait_ge(share_ready, SHARES * j)
                    dve.wait_ge(mix_copied, j)
                    positive(dve, out_ready, j - 1)
                    nc.vector.tensor_tensor(scaled[:], share[:], mixed[old % 2][:], ALU.mult).then_inc(scaled_ready, 1)
                row_maximum(7)
                if job(1):
                    tops, minus = top[nxt % 2], minus_top[nxt % 2]
                    dve.wait_ge(row_max, MT * (j + 2))
                    positive(dve, top_rows, j)
                    nc.vector.tensor_scalar(minus[:, :, HIGH_ROW], tops[:], -1.0, None, ALU.mult).then_inc(top_high, 1)
                    dve.wait_ge(top_high, j + 2)
                    nc.vector.scalar_tensor_tensor(minus[:, :, LOW_ROW], tops[:], -1.0, minus[:, :, HIGH_ROW],
                                                   ALU.mult, ALU.subtract).then_inc(top_low, 1)
                    dve.wait_ge(top_rows, j + 2)
                    rows = slice(64, P)
                    nc.vector.tensor_tensor(q[nxt][rows, :], misc_ps[rows, :], q[nxt][rows, :],
                                            ALU.add).then_inc(top_added, 1)
                if job(-1):
                    dve.wait_ge(scaled_ready, j)
                    stores = 16 * ((DEEP // 2) * i + (u - 1) // 2)
                    positive(dve, out_stored[old % 2], stores)
                    nc.vector.scalar_tensor_tensor(out[old % 2][:], scaled[:], bv_col[:], x[old][:],
                                                   ALU.add, ALU.add).then_inc(out_ready, 1)

            pipeline(dve, part)

        @block.scalar
        def _(act):
            act.wait_ge(weights_in, 16 * WEIGHTS)
            act.wait_ge(ident_turn, 6)

            def part(i, u, job):
                j = DEEP * i + u
                new = (u + 2) % DEEP

                def exponentials(t):
                    if not job(0):
                        return
                    tile = probs[t % PROBS]
                    for h in range(HALVES):
                        act.wait_ge(keys_ready, (MT * j + t) * HALVES + h + 1)
                        if h == 0:
                            positive(act, probs_mixed, MT * j + t - PROBS + 1)
                            if t >= PROBS:
                                before = (MT - 1) * j + (t - PROBS if t > PROBS else 1)
                            else:
                                before = (MT - 1) * (j - 1) + MT - PROBS + t
                            positive(act, probs_summed, before)
                        half = slice(h * BANK, (h + 1) * BANK)
                        nc.scalar.activation(tile[:, half], keys_ps[:, half], ACT.Exp).then_inc(probs_ready, 1)

                exponentials(0)
                if job(-1):
                    act.wait_ge(probs_mixed, MT * j)
                    positive(act, scaled_ready, j - 2)
                    nc.scalar.activation(mixed[(u - 1) % 2][:], mix_ps[:], ACT.Copy).then_inc(mix_copied, 1)
                exponentials(1)
                if job(-1):
                    act.wait_ge(sum_rows, j)
                    positive(act, scaled_ready, j - 1)
                    nc.scalar.activation(share[:], misc_ps[:], ACT.Copy).then_inc(sum_copied, 1)
                exponentials(2)
                if job(2):
                    act.wait_ge(k_proj, j + 3)
                    nc.scalar.activation(k[new][:], misc_ps[:], ACT.Identity, bias=bk_rows[:]).then_inc(k_high, 1)
                exponentials(3)
                if job(2):
                    act.wait_ge(q_proj, j + 3)
                    nc.scalar.activation(q[new][:], misc_ps[:], ACT.Identity, bias=bq_rows[:]).then_inc(q_high, 1)
                exponentials(4)
                if job(2):
                    act.wait_ge(v_proj, j + 3)
                    nc.scalar.activation(v[new][:].rearrange("p t c -> p (t c)"), misc_ps[:],
                                         ACT.Copy).then_inc(v_ready, 1)
                for t in range(5, MT):
                    exponentials(t)

            pipeline(act, part)

        @block.tensor
        def _(pe):
            pe.wait_ge(weights_in, 16 * WEIGHTS)
            pe.wait_ge(ident_turn, 6)

            def part(i, u, job):
                j = DEEP * i + u
                cur, nxt, new, old = u % DEEP, (u + 1) % DEEP, (u + 2) % DEEP, (u - 1) % DEEP

                def key_energies(t):
                    if not job(0):
                        return
                    if t == 0:
                        pe.wait_ge(top_added, j + 1)
                    for h in range(HALVES):
                        half = slice(h * BANK, (h + 1) * BANK)
                        positive(pe, probs_ready, (MT * j + t - 1) * HALVES + h + 1)
                        nc.tensor.matmul(keys_ps[:, half], k[cur][:, t * P:(t + 1) * P], q[cur][:, half],
                                         start=True, stop=True).then_inc(keys_ready, 1)

                def row_energies(t):
                    if not job(1):
                        return
                    if t == 0:
                        pe.wait_ge(k_low, j + 2)
                        pe.wait_ge(q_low, j + 2)
                    positive(pe, row_max, MT * (j + 1) + t)
                    for h in range(HALVES):
                        half = slice(h * BANK, (h + 1) * BANK)
                        mm = nc.tensor.matmul(rows_ps[:, half], q[nxt][:, t * P:(t + 1) * P], k[nxt][:, half],
                                              start=True, stop=True)
                    mm.then_inc(rows_ready, 1)

                def mix(t, h):
                    if not job(0):
                        return
                    if t == 0 and h == 0:
                        pe.wait_ge(v_ready, j + 1)
                        positive(pe, mix_copied, j)
                    half = slice(h * BANK, (h + 1) * BANK)
                    pe.wait_ge(probs_ready, (MT * j + t) * HALVES + h + 1)
                    mm = nc.tensor.matmul(mix_ps[:, half], v[cur][:, t, :], probs[t % PROBS][:, half],
                                          start=(t == 0), stop=(t == MT - 1))
                    if h == HALVES - 1:
                        mm.then_inc(probs_mixed, 1)

                def project(weights, done):
                    for h in range(HALVES):
                        half = slice(h * BANK, (h + 1) * BANK)
                        mm = nc.tensor.matmul(misc_ps[:, half], weights[:], x[new][:, half], start=True, stop=True)
                    mm.then_inc(done, 1)

                def sum_probabilities():
                    if not job(-1):
                        return
                    pe.wait_ge(probs_summed, (MT - 1) * j)
                    if job(0):
                        pe.wait_ge(top_added, j + 1)
                    else:
                        pe.wait_ge(sum_copied, j - 1)
                    for h in range(HALVES):
                        half = slice(h * BANK, (h + 1) * BANK)
                        mm = nc.tensor.matmul(misc_ps[:, half], ones[:], psum_keys[old % 2][:, half],
                                              start=True, stop=True)
                    mm.then_inc(sum_rows, 1)

                def project_k():
                    if job(2):
                        pe.wait_ge(x_in[new], 16 * i + 16 * ((u + 2) // DEEP + 1))
                        positive(pe, v_ready, j + 2)
                        positive(pe, sum_copied, j)
                        positive(pe, top_added, j + 1)
                        project(wk_rows, k_proj)

                def project_q():
                    if job(2):
                        pe.wait_ge(k_low, j + 3)
                        project(wq_rows, q_proj)

                def project_v():
                    if job(2):
                        pe.wait_ge(q_low, j + 3)
                        for t in range(MT):
                            mm = nc.tensor.matmul(misc_ps[:, t * P:(t + 1) * P], x[new][:, t * P:(t + 1) * P],
                                                  wv_sb[:], start=True, stop=True)
                        mm.then_inc(v_proj, 1)

                beside = {1: sum_probabilities, 2: project_k, 3: project_q, 4: project_v}
                for t in range(MT):
                    key_energies(t)
                    row_energies(t)
                    if t in beside:
                        beside[t]()
                    if t > 0:
                        mix(t - 1, 0)
                        mix(t - 1, 1)
                if job(1):
                    pe.wait_ge(top_low, j + 2)
                    pe.wait_ge(v_ready, j + 3) if job(2) else None
                    for t in range(MT):
                        mm = nc.tensor.matmul(misc_ps[:, t * P:(t + 1) * P], minus_top[nxt % 2][:, t, :], ident_r[:],
                                              start=True, stop=True)
                    mm.then_inc(top_rows, 1)
                mix(MT - 1, 0)
                mix(MT - 1, 1)

            pipeline(pe, part)


def build(nc, t):
    with ExitStack() as ctx:
        psum = [ctx.enter_context(nc.psum_tensor(f"psum{n}", [P, CELLS], F32)) for n in range(4)]
        layers(nc, ctx, psum, t)


def layers(nc, sems, psum, t):
    inner = [nc.dram_tensor(f"layer{n}_out", [BATCH, P, CELLS], F32, kind="Internal").ap() for n in range(3)]
    scan_layer(nc, sems, "L0", psum, t["x_cells"], inner[0], *(t[f"L0_conv_{n}"] for n in ("w1", "b1", "w2", "b2", "w_y")))
    attention_layer(nc, sems, "L1", psum, inner[0], inner[1],
                    *(t[f"L1_conv_{n}"] for n in ("Wq", "bq", "Wk", "bk", "Wv", "bv", "gamma")))
    attention_layer(nc, sems, "L2", psum, inner[1], inner[2],
                    *(t[f"L2_conv_{n}"] for n in ("wq", "bq", "wk", "bk", "wv", "bv")), None)
    scan_layer(nc, sems, "L3", psum, inner[2], t["y_cells"], *(t[f"L3_conv_{n}"] for n in ("w1", "b1", "w2", "b2", "w_y")))


def kernel(**inputs):
    import concourse.bacc as bacc
    from concourse.bass_utils import run_bass_kernel_spmd

    arrays = {n: np.asarray(a) for n, a in inputs.items()}
    x = arrays.pop("x").reshape(BATCH, CELLS, P)[:, GRID, :]
    arrays["x_cells"] = np.ascontiguousarray(x.transpose(0, 2, 1))
    for n in ("L0_conv_b2", "L3_conv_b2", "L1_conv_gamma"):
        arrays[n] = arrays[n].reshape(1, 1)
    nc = bacc.Bacc("TRN2", target_bir_lowering=False, num_devices=1)
    t = {n: nc.dram_tensor(n, a.shape, F32, kind="ExternalInput").ap() for n, a in arrays.items()}
    t["y_cells"] = nc.dram_tensor("y_cells", [BATCH, P, CELLS], F32, kind="ExternalOutput").ap()
    build(nc, t)
    got = run_bass_kernel_spmd(nc, [arrays], core_ids=[0]).results[0]["y_cells"]
    y = np.empty((BATCH, CELLS, P), np.float32)
    y[:, GRID, :] = got.transpose(0, 2, 1)
    return y.reshape(BATCH, SIDE, SIDE, P)
```

```python
from contextlib import ExitStack

import numpy as np

import concourse.bass as bass
from concourse import mybir

F32 = mybir.dt.float32
F32R = mybir.dt.float32r
ALU = mybir.AluOpType
ACT = mybir.ActivationFunctionType
AX_X = mybir.AxisListType.X

P = 128
SIDE = 32
CELLS = SIDE * SIDE
BATCH = 64
HID = 256
DQK = 16
BANK = 512



def spiral_path():
    cy = cx = SIDE // 2
    path, seen = [], set()

    def visit(ring, y, x):
        if 0 <= y < SIDE and 0 <= x < SIDE and (y, x) not in seen:
            seen.add((y, x))
            path.append((ring, y, x))

    visit(0, cy, cx)
    for r in range(1, SIDE // 2 + 1):
        top, bottom, left, right = cy - r, cy + r, cx - r, cx + r
        for x in range(left, right + 1):
            visit(r, top, x)
        for y in range(top + 1, bottom + 1):
            visit(r, y, right)
        for x in range(right - 1, left - 1, -1):
            visit(r, bottom, x)
        for y in range(bottom - 1, top, -1):
            visit(r, y, left)
    return path


LATE, OLD, NEW, STEP, EDGE = range(5)


def neighbours(y, x):
    near = ((y - 1, x), (y + 1, x), (y, x - 1), (y, x + 1))
    return [(a, b) for a, b in near if 0 <= a < SIDE and 0 <= b < SIDE]


def wavefront():
    path = spiral_path()
    rank = {(y, x): n for n, (_, y, x) in enumerate(path)}
    level, ring = {}, {}
    for n, (r, y, x) in enumerate(path):
        earlier = [level[c] for c in neighbours(y, x) if rank[c] < n]
        level[y, x] = max(earlier, default=-1 if (y, x) != (0, 0) else 0) + 1
        ring[y, x] = r
    ending = {path[n][1:] for n in range(1, CELLS) if n + 1 == CELLS or path[n + 1][0] != path[n][0]}
    order = sorted(level, key=lambda c: (c in ending, level[c], ring[c]))
    at = {c: n for n, c in enumerate(order)}
    levels = max(level.values()) + 1
    members = [[c for c in order if level[c] == lv] for lv in range(levels)]
    starts = [sum(len([c for c in m if c not in ending]) for m in members[:lv]) for lv in range(levels + 1)]
    ends = [next((at[c] for c in m if c in ending), None) for m in members]

    sums_late, sums_old, sums_new, steps, edges = [], [], [], [], []
    first_read, last_read = [level[c] for c in order], [level[c] for c in order]
    for lv, cells in enumerate(members):
        ops = {kind: [] for kind in (LATE, OLD, NEW, STEP, EDGE)}
        by_turn = {}

        def run(kind, key, n, a, b):
            if ops[kind] and ops[kind][-1][0] == key:
                _, n0, k, a0, b0 = ops[kind][-1]
                follows = all((s is None) == (s0 is None) and (s is None or s == s0 + k)
                              for s, s0 in ((a, a0), (b, b0)))
                if n == n0 + k and follows:
                    ops[kind][-1] = (key, n0, k + 1, a0, b0)
                    return
            ops[kind].append((key, n, 1, a, b))

        for n, c in enumerate(cells):
            near = neighbours(*c)
            late = sorted((d for d in near if rank[d] > rank[c]), key=rank.get, reverse=True)
            early = sorted((d for d in near if rank[d] < rank[c]), key=rank.get)
            old = [d for d in early if level[d] < lv - 1]
            new = [d for d in early if level[d] == lv - 1]
            assert all(level[d] > lv for d in late) and len(late + old) > 0 and len(late + old + new) == len(near)
            for d in near:
                first_read[at[d]] = min(first_read[at[d]], lv)
                last_read[at[d]] = max(last_read[at[d]], lv)
            terms = ([(at[d], LATE, t) for t, d in enumerate(late)] + [(at[d], OLD, t) for t, d in enumerate(old)]
                     + [(at[d], NEW, t) for t, d in enumerate(new, 4 - len(new))])
            (a, _, _), (b, kind, t) = terms[:2]
            by_turn.setdefault((kind, t), []).append((n, a, b))
            for a, kind, t in terms[2:]:
                by_turn.setdefault((kind, t), []).append((n, None, a))
            if len(near) < 4:
                by_turn.setdefault((EDGE, len(near)), []).append((n, None, None))
            for t, d in enumerate(new, 4 - len(new)):
                by_turn.setdefault((STEP, (t, 4 / len(near))), []).append((n, None, members[lv - 1].index(d)))
        for (kind, turn), terms in sorted(by_turn.items()):
            for n, a, b in terms:
                run(kind, turn, n, a, b)
        for kind, out in ((LATE, sums_late), (OLD, sums_old), (NEW, sums_new)):
            out.append([o[1:] for o in ops[kind]])
        steps.append([(n, k, b, factor) for (_, factor), n, k, _, b in ops[STEP]])
        edges.append([(n, k, count) for count, n, k, _, _ in ops[EDGE]])
    grid = np.array([y * SIDE + x for y, x in order])
    return grid, starts, ends, sums_late, sums_old, sums_new, steps, edges, first_read, last_read


GRID, STARTS, ENDS, SUMS_LATE, SUMS_OLD, SUMS_NEW, STEPS, EDGES, FIRST_READ, LAST_READ = wavefront()
LEVELS = len(STARTS) - 1


def chunk_levels():
    first = [0, 2]
    for lv in range(2, LEVELS):
        if STARTS[lv + 1] - STARTS[first[-1]] > CELLS // 8 and lv > first[-1]:
            first.append(lv)
    return first + [LEVELS]


CHUNKS = chunk_levels()
ENDING = len(CHUNKS) - 1


def level_size(lv):
    return STARTS[lv + 1] - STARTS[lv] + (ENDS[lv] is not None)


def chunk_cells(k):
    return slice(STARTS[-1], CELLS) if k == ENDING else slice(STARTS[CHUNKS[k]], STARTS[CHUNKS[k + 1]])


def positive(engine, semaphore, value):
    if not isinstance(value, int) or value > 0:
        engine.wait_ge(semaphore, value)



def scan_layer(nc, sems, tag, psum, src, dst, w1, b1, w2, b2, w_y):
    IMAGES = 32
    ROUNDS = BATCH // IMAGES
    HALVES = HID // P
    WIDE = max(level_size(lv) for lv in range(LEVELS))
    assert WIDE * IMAGES <= BANK
    NC = ENDING + 1

    with ExitStack() as ctx:
        sb = lambda name, shape, dt=F32: ctx.enter_context(nc.sbuf_tensor(f"{tag}_{name}", shape, dt))
        sem = lambda name: sems.enter_context(nc.semaphore(f"{tag}_{name}"))

        x = sb("x", [P, IMAGES, CELLS])
        near = [sb(f"near{k}", [P, IMAGES, WIDE]) for k in range(2)]
        hidden = [sb(f"hidden{h}", [P, IMAGES, WIDE]) for h in range(HALVES)]
        w1_own = sb("w1_own", [P, HID])
        w1_near = sb("w1_near", [P, HID])
        w1_sum = sb("w1_sum", [P, HID])
        b1_col = sb("b1_col", [P, HALVES])
        w2_col = sb("w2_col", [P, HALVES])
        wy_rows = sb("wy_rows", [P, P])
        wy_col = sb("wy_col", [P, 1])
        b2_col = sb("b2_col", [P, 1])
        b2wy = sb("b2wy", [P, 1])
        w2wy = [sb(f"w2wy{h}", [P, P]) for h in range(HALVES)]
        pre = [[psum[k][:, h * BANK:(h + 1) * BANK] for h in range(HALVES)] for k in range(2)]
        step = [psum[2][:, k * BANK:(k + 1) * BANK] for k in range(2)]

        weights_in = sem("weights_in")
        weights_ready = sem("weights_ready")
        loaded = [sem(f"loaded{k}") for k in range(NC)]
        stored = [sem(f"stored{k}") for k in range(NC)]
        late_ready = sem("late_ready")
        near_turn = sem("near_turn")
        pre_ready = sem("pre_ready")
        tanh_ready = sem("tanh_ready")
        step_ready = sem("step_ready")
        updated = sem("updated")
        block = ctx.enter_context(nc.Block())

        def images(r):
            return slice(r * IMAGES, (r + 1) * IMAGES)

        def cells(t, lv):
            return t[:, :, 0:level_size(lv)]

        def columns(t, lv, o=0, k=None):
            n = level_size(lv)
            return t[:, 0:IMAGES * n].rearrange("p (b n) -> p b n", b=IMAGES)[:, :, o:o + (n if k is None else k)]

        def own_parts(lv):
            n = STARTS[lv + 1] - STARTS[lv]
            return [(0, n, STARTS[lv])] * (n > 0) + ([(n, 1, ENDS[lv])] if ENDS[lv] is not None else [])

        def wait_loads(engine, lv, r, first_use):
            for k in range(NC):
                if min(first_use[chunk_cells(k)]) == lv:
                    engine.wait_ge(loaded[k], 16 * (r + 1))

        own_level = [lv for lv in range(LEVELS) for _ in range(STARTS[lv], STARTS[lv + 1])]
        own_level += [lv for lv in range(LEVELS) if ENDS[lv] is not None]

        def late_count(lv):
            return sum(len(SUMS_LATE[v]) for v in range(lv))

        def turn_count(lv):
            return sum(len(kind[v]) for kind in (SUMS_OLD, SUMS_NEW, EDGES, STEPS) for v in range(lv))

        LATE_ROUND, TURN_ROUND = late_count(LEVELS), turn_count(LEVELS)
        assert turn_count(1) == 0

        def load(sp, r, k):
            sp.dma_start(x[:, :, chunk_cells(k)], src[images(r), :, chunk_cells(k)].rearrange("b c n -> c b n")
                         ).then_inc(loaded[k], 16)

        def reload(sp, r, k):
            sp.wait_ge(stored[k], 16 * (r + 1))
            sp.wait_ge(updated, r * LEVELS + max(LAST_READ[chunk_cells(k)]) + 1)
            load(sp, r + 1, k)

        @block.sync
        def _(sp):
            with nc.allow_non_contiguous_dma(reason="small weight columns"):
                for dram, tile in ((w1[0:P, :], w1_own[:]), (w1[P:2 * P, :], w1_near[:]),
                                   (b1.rearrange("(h p) -> p h", p=P), b1_col[:]),
                                   (w2.rearrange("(h p) -> p h", p=P), w2_col[:]),
                                   (w_y.rearrange("(a c) -> a c", a=1).to_broadcast([P, P]), wy_rows[:]),
                                   (w_y.rearrange("(c a) -> c a", a=1), wy_col[:]),
                                   (b2.to_broadcast([P, 1]), b2_col[:])):
                    sp.dma_start(tile, dram).then_inc(weights_in, 16)
                for k in (ENDING, *range(ENDING)):
                    load(sp, 0, k)
                def store(r, k):
                    sp.wait_ge(updated, r * LEVELS + max(own_level[chunk_cells(k)]) + 1)
                    sp.dma_start(dst[images(r), :, chunk_cells(k)].rearrange("b c n -> c b n"),
                                 x[:, :, chunk_cells(k)]).then_inc(stored[k], 16)

                for r in range(ROUNDS):
                    more = r + 1 < ROUNDS
                    for k in range(ENDING - 1):
                        store(r, k)
                        if more and k >= 2:
                            reload(sp, r, k - 1)
                    if more:
                        reload(sp, r, 0)
                    store(r, ENDING)
                    if more:
                        reload(sp, r, ENDING)
                        reload(sp, r, ENDING - 2)
                    store(r, ENDING - 1)
                    if more:
                        reload(sp, r, ENDING - 1)
                for k in range(NC):
                    sp.wait_ge(stored[k], 16 * ROUNDS)

        @block.gpsimd
        def _(pool):
            with pool.Fori(0, ROUNDS) as r:
                for lv in range(LEVELS):
                    wait_loads(pool, lv, r, FIRST_READ)
                    if lv >= 2:
                        pool.wait_ge(pre_ready, (r * LEVELS + lv - 1) * HALVES)
                    for n, (o, k, s0, s1) in enumerate(SUMS_LATE[lv]):
                        out = near[lv % 2][:, :, o:o + k]
                        if s0 is None:
                            pool.wait_ge(late_ready, r * LATE_ROUND + late_count(lv) + n)
                        in0 = out if s0 is None else x[:, :, s0:s0 + k]
                        nc.gpsimd.tensor_tensor(out, in0, x[:, :, s1:s1 + k], ALU.add).then_inc(late_ready, 1)

        @block.vector
        def _(dve):
            dve.wait_ge(weights_in, 16 * 7)
            nc.vector.tensor_scalar(w1_sum[:], w1_near[:], 0.25, None, ALU.mult).then_inc(weights_ready, 1)
            nc.vector.tensor_tensor(b2wy[:], b2_col[:], wy_col[:], ALU.mult).then_inc(weights_ready, 1)
            for h in range(HALVES):
                nc.vector.tensor_scalar(w2wy[h][:], wy_rows[:], w2_col[:, h:h + 1], None,
                                        ALU.mult).then_inc(weights_ready, 1)
            dve.wait_ge(weights_ready, 2 + HALVES)

            def sum_before_step(lv, r):
                dve.wait_ge(late_ready, r * LATE_ROUND + late_count(lv + 1))
                turn = r * TURN_ROUND + turn_count(lv)
                if SUMS_OLD[lv]:
                    dve.wait_ge(updated, r * LEVELS + lv - 1)
                n = 0
                for op in (*SUMS_OLD[lv], *SUMS_NEW[lv]):
                    o, k, s0, s1 = op
                    out = near[lv % 2][:, :, o:o + k]
                    if s0 is None and n > 0:
                        dve.wait_ge(near_turn, turn + n)
                    in0 = out if s0 is None else x[:, :, s0:s0 + k]
                    if n < len(SUMS_OLD[lv]):
                        nc.vector.tensor_tensor(out, in0, x[:, :, s1:s1 + k], ALU.add).then_inc(near_turn, 1)
                    else:
                        nc.vector.scalar_tensor_tensor(out, x[:, :, s1:s1 + k], b2wy[:], in0,
                                                       ALU.add, ALU.add).then_inc(near_turn, 1)
                    n += 1
                for o, k, count in EDGES[lv]:
                    out = near[lv % 2][:, :, o:o + k]
                    if n > 0:
                        dve.wait_ge(near_turn, turn + n)
                    nc.vector.tensor_scalar(out, out, 4.0 / count, None, ALU.mult).then_inc(near_turn, 1)
                    n += 1
                return turn, n

            def add_steps(lv, turn, n):
                dve.wait_ge(near_turn, turn + n)
                written = set()
                for o, k, s1, factor in STEPS[lv]:
                    if written & set(range(o, o + k)):
                        dve.wait_ge(near_turn, turn + n)
                    written |= set(range(o, o + k))
                    out = near[lv % 2][:, :, o:o + k]
                    nc.vector.scalar_tensor_tensor(out, columns(step[(lv - 1) % 2], lv - 1, s1, k), factor, out,
                                                   ALU.mult, ALU.add).then_inc(near_turn, 1)
                    n += 1

            with dve.Fori(0, ROUNDS) as r:
                for lv in range(LEVELS):
                    if lv + 1 < LEVELS:
                        done = sum_before_step(lv + 1, r)
                    dve.wait_ge(step_ready, r * LEVELS + lv + 1)
                    if lv + 1 < LEVELS:
                        add_steps(lv + 1, *done)
                    for o, k, position in own_parts(lv):
                        own = x[:, :, position:position + k]
                        ins = nc.vector.scalar_tensor_tensor(own, columns(step[lv % 2], lv, o, k), b2wy[:], own,
                                                             ALU.add, ALU.add)
                    ins.then_inc(updated, 1)

        @block.scalar
        def _(act):
            act.wait_ge(weights_in, 16 * 7)
            with act.Fori(0, ROUNDS) as r:
                for lv in range(LEVELS):
                    for h in range(HALVES):
                        act.wait_ge(pre_ready, (r * LEVELS + lv) * HALVES + h + 1)
                        nc.scalar.activation(cells(hidden[h], lv), columns(pre[lv % 2][h], lv),
                                             ACT.Tanh, bias=b1_col[:, h:h + 1]).then_inc(tanh_ready, 1)

        @block.tensor
        def _(pe):
            pe.wait_ge(weights_ready, 2 + HALVES)

            def own_products(lv, r):
                wait_loads(pe, lv, r, own_level)
                for h in range(HALVES):
                    for n, (o, k, position) in enumerate(own_parts(lv)):
                        nc.tensor.matmul(columns(pre[lv % 2][h], lv, o, k), w1_own[:, h * P:(h + 1) * P],
                                         x[:, :, position:position + k], start=(n == 0), stop=False,
                                         skip_group_check=True)

            with pe.Fori(0, ROUNDS) as r:
                own_products(0, r)
                for lv in range(LEVELS):
                    if lv == 0:
                        pe.wait_ge(late_ready, r * LATE_ROUND + late_count(1))
                    else:
                        pe.wait_ge(near_turn, r * TURN_ROUND + turn_count(lv + 1))
                    for h in range(HALVES):
                        nc.tensor.matmul(columns(pre[lv % 2][h], lv), w1_sum[:, h * P:(h + 1) * P],
                                         cells(near[lv % 2], lv), start=False, stop=True,
                                         skip_group_check=True).then_inc(pre_ready, 1)
                    for h in range(HALVES):
                        pe.wait_ge(tanh_ready, (r * LEVELS + lv) * HALVES + h + 1)
                        mm = nc.tensor.matmul(columns(step[lv % 2], lv), w2wy[h][:], cells(hidden[h], lv),
                                              start=(h == 0), stop=(h == HALVES - 1))
                    mm.then_inc(step_ready, 1)
                    if lv + 1 < LEVELS:
                        own_products(lv + 1, r)



def attention_layers(nc, sems, tag, psum, arrays, weights):
    LAYERS = len(weights)
    MT = CELLS // P
    HALVES = CELLS // BANK
    DEEP = 4
    PROBS = 4
    DIAGONAL_AFTER = 0
    LOW_ROW, HIGH_ROW = 80, 96

    with ExitStack() as ctx:
        sb = lambda name, shape, dt=F32: ctx.enter_context(nc.sbuf_tensor(f"{tag}_{name}", shape, dt))
        sem = lambda name: sems.enter_context(nc.semaphore(f"{tag}_{name}"))

        x = [sb(f"x{u}", [P, CELLS]) for u in range(DEEP)]
        q = [sb(f"q{u}", [P, CELLS], F32R) for u in range(DEEP)]
        k = [sb(f"k{u}", [P, CELLS], F32R) for u in range(DEEP)]
        v_high = [sb(f"v_high{u}", [P, CELLS], F32R) for u in range(DEEP)]
        v_low = [sb(f"v_low{u}", [P, CELLS], F32R) for u in range(DEEP)]
        probs = [sb(f"probs{n}", [P, CELLS]) for n in range(PROBS)]
        probs_high = [sb(f"probs_high{n}", [P, CELLS], F32R) for n in range(PROBS)]
        probs_low = [sb(f"probs_low{n}", [P, CELLS], F32R) for n in range(PROBS)]
        row_probs = sb("row_probs", [P, CELLS])
        mixed = [sb(f"mixed{u}", [P, CELLS]) for u in range(2)]
        scaled = sb("scaled", [P, CELLS])
        out = [sb(f"out{u}", [P, CELLS]) for u in range(2)]
        half_top = [sb(f"half_top{u}", [P, HALVES * MT]) for u in range(2)]
        half_sum = [sb(f"half_sum{u}", [P, HALVES * MT]) for u in range(2)]
        rescale = sb("rescale", [P, HALVES * MT])
        top = [sb(f"top{u}", [P, MT]) for u in range(2)]
        row_sum = sb("row_sum", [P, MT])
        minus_top = [sb(f"minus_top{u}", [P, MT, P], F32R) for u in range(2)]
        share = sb("share", [P, MT])
        share_high, share_low = sb("share_high", [P, MT], F32R), sb("share_low", [P, MT], F32R)
        high_diagonal = [sb(f"high_diagonal{u}", [P, CELLS], F32R) for u in range(2)]
        low_diagonal = [sb(f"low_diagonal{u}", [P, CELLS], F32R) for u in range(2)]
        ones = sb("ones", [P, P])
        per_layer = lambda name, columns: [sb(f"{name}{n}", [P, columns]) for n in range(LAYERS)]
        wq_rows, wk_rows, wv_sb = per_layer("wq_rows", P), per_layer("wk_rows", P), per_layer("wv_sb", P)
        bq_rows, bk_rows, bv_col = per_layer("bq_rows", 1), per_layer("bk_rows", 1), per_layer("bv_col", 1)
        gamma_col = per_layer("gamma_col", 1)
        ident = sb("ident", [P, P])
        ident_r = sb("ident_r", [P, P], F32R)
        ones_r = sb("ones_r", [P, P], F32R)

        rows_ps, keys_ps, mix_ps, misc_ps = psum

        weights_in = [sem(f"weights_in{n}") for n in range(LAYERS)]
        consts_ready, ident_turn = sem("consts_ready"), sem("ident_turn")
        setup_done = sem("setup_done")
        x_in = [sem(f"x_in{u}") for u in range(DEEP)]
        out_stored = [sem(f"out_stored{u}") for u in range(2)]
        k_proj, q_proj, v_proj = sem("k_proj"), sem("q_proj"), sem("v_proj")
        k_high, q_high, v_ready = sem("k_high"), sem("q_high"), sem("v_ready")
        k_low, q_low = sem("k_low"), sem("q_low")
        rows_ready, row_max, row_summed = sem("rows_ready"), sem("row_max"), sem("row_summed")
        top_ready, rescale_turn = sem("top_ready"), sem("rescale_turn")
        top_high, top_low, top_rows, top_added = (sem(n) for n in ("top_high", "top_low", "top_rows", "top_added"))
        keys_ready, probs_ready = sem("keys_ready"), sem("probs_ready")
        high_ready, low_ready = sem("high_ready"), sem("low_ready")
        probs_mixed, v_low_ready = sem("probs_mixed"), sem("v_low_ready")
        mix_copied = sem("mix_copied")
        share_ready, diagonal_ready, share_rows = sem("share_ready"), sem("diagonal_ready"), sem("share_rows")
        scaled_ready, out_ready = sem("scaled_ready"), sem("out_ready")
        block = ctx.enter_context(nc.Block())

        scaled_values = [n for n in range(LAYERS) if weights[n][-1] is not None]
        WEIGHTS = [14 + (n in scaled_values) for n in range(LAYERS)]
        CONSTS = 5 * LAYERS + 1 + 2
        SETUP = 2 + 2 * len(scaled_values)

        def pipeline(engine, part):
            GROUPS = BATCH // DEEP

            def group(i, n, steps):
                for u in steps:
                    image = lambda d: DEEP * i + u + d
                    job = lambda d: not isinstance(i, int) or 0 <= image(d) < LAYERS * BATCH
                    layer = lambda d: image(d) // BATCH if isinstance(i, int) else n
                    part(i, u, job, layer)

            for n in range(LAYERS):
                group(GROUPS * n, n, range(-2 if n == 0 else 0, DEEP))
                with engine.Fori(GROUPS * n + 1, GROUPS * (n + 1) - 1) as i:
                    group(i, n, range(DEEP))
                if n + 1 < LAYERS:
                    engine.wait_ge(weights_in[n + 1], 16 * WEIGHTS[n + 1])
                group(GROUPS * (n + 1) - 1, n, range(DEEP + (n == LAYERS - 1)))

        def load_weights(engine):
            engine.wait_ge(consts_ready, CONSTS)
            with nc.allow_non_contiguous_dma(reason="small weight columns"):
                for n, (wq, bq, wk, bk, wv, bv, gamma) in enumerate(weights):
                    for g in range(3):
                        rows = slice(32 * g, 32 * g + DQK)
                        engine.dma_start(wq_rows[n][:, rows], wq).then_inc(weights_in[n], 16)
                        engine.dma_start(wk_rows[n][:, rows], wk).then_inc(weights_in[n], 16)
                        engine.dma_start(bq_rows[n][rows, :], bq.rearrange("(d a) -> d a", a=1)).then_inc(weights_in[n], 16)
                        engine.dma_start(bk_rows[n][rows, :], bk.rearrange("(d a) -> d a", a=1)).then_inc(weights_in[n], 16)
                    engine.dma_start(wv_sb[n][:], wv).then_inc(weights_in[n], 16)
                    engine.dma_start(bv_col[n][:], bv.rearrange("(c a) -> c a", a=1)).then_inc(weights_in[n], 16)
                    if gamma is not None:
                        engine.dma_start(gamma_col[n][:], gamma.to_broadcast([P, 1])).then_inc(weights_in[n], 16)

        @block.sync
        def _(sp):
            sp.dma_start(x[0][:], arrays[0][0, :, :]).then_inc(x_in[0], 16)
            load_weights(sp)

            def image_of(array, n):
                return array[bass.ds(n, 1), :, :].rearrange("b c n -> c (b n)")

            def part(i, u, job, layer):
                j = DEEP * i + u
                if job(3):
                    n = layer(3)
                    positive(sp, out_ready, j)
                    if n > 0:
                        sp.wait_ge(out_stored[(u + 3) % 2],
                                   16 * ((DEEP // 2) * i + (u + 3) // 2 - BATCH // 2 + 1))
                    sp.dma_start(x[(u + 3) % DEEP][:], image_of(arrays[n], j + 3 - n * BATCH)
                                 ).then_inc(x_in[(u + 3) % DEEP], 16)
                if job(-1):
                    n = layer(-1)
                    sp.wait_ge(out_ready, j)
                    sp.dma_start(image_of(arrays[n + 1], j - 1 - n * BATCH),
                                 out[(u - 1) % 2][:]).then_inc(out_stored[(u - 1) % 2], 16)

            pipeline(sp, part)
            for u in range(2):
                sp.wait_ge(out_stored[u], 16 * LAYERS * BATCH // 2)

        @block.gpsimd
        def _(pool):
            for n in range(LAYERS):
                nc.gpsimd.memset(wq_rows[n][:], 0.0).then_inc(consts_ready, 1)
                nc.gpsimd.memset(wk_rows[n][:], 0.0).then_inc(consts_ready, 1)
                nc.gpsimd.memset(bq_rows[n][:], 0.0).then_inc(consts_ready, 1)
                nc.gpsimd.memset(bk_rows[n][:], 0.0).then_inc(ident_turn, 1)
            nc.gpsimd.memset(ones[:], 1.0).then_inc(consts_ready, 1)
            nc.gpsimd.memset(ident[:], 0.0).then_inc(ident_turn, 1)
            pool.wait_ge(ident_turn, LAYERS + 1)
            nc.gpsimd.affine_select(out=ident[:], in_=ident[:], compare_op=ALU.not_equal, fill=1.0,
                                    base=0, pattern=[[-1, P]], channel_multiplier=1).then_inc(ident_turn, 1)
            for turn, row in enumerate((LOW_ROW, HIGH_ROW)):
                pool.wait_ge(ident_turn, LAYERS + 2 + turn * LAYERS)
                for n in range(LAYERS):
                    done = consts_ready if row == HIGH_ROW else ident_turn
                    nc.gpsimd.affine_select(out=bk_rows[n][:], in_=bk_rows[n][:], compare_op=ALU.not_equal, fill=1.0,
                                            base=-row, pattern=[[0, 1]], channel_multiplier=1).then_inc(done, 1)
            for n in range(LAYERS):
                nc.gpsimd.memset(gamma_col[n][:], 1.0).then_inc(consts_ready, 1)

            def part(i, u, job, layer):
                j = DEEP * i + u
                if not job(0):
                    return
                for t in range(MT):
                    pool.wait_ge(high_ready, MT * j + t + 1)
                    positive(pool, probs_mixed, MT * j + t - PROBS + 1)
                    nc.gpsimd.tensor_tensor(probs_low[t % PROBS][:], probs[t % PROBS][:], probs_high[t % PROBS][:],
                                            ALU.subtract).then_inc(low_ready, 1)
                    if t == DIAGONAL_AFTER:
                        pool.wait_ge(share_ready, 4 * j + 4)
                        positive(pool, share_rows, j - 1)
                        for diagonal, values in ((high_diagonal, share_high), (low_diagonal, share_low)):
                            nc.gpsimd.tensor_tensor(diagonal[u % 2][:].rearrange("p (t c) -> p t c", t=MT),
                                                    ident[:].unsqueeze(1).to_broadcast([P, MT, P]),
                                                    values[:].unsqueeze(2).to_broadcast([P, MT, P]), ALU.mult
                                                    ).then_inc(diagonal_ready, 1)

            pipeline(pool, part)

        @block.vector
        def _(dve):
            for u in range(2):
                nc.vector.memset(minus_top[u][:].bitcast(F32), 0.0).then_inc(consts_ready, 1)
            dve.wait_ge(consts_ready, CONSTS)
            nc.vector.tensor_copy(ident_r[:], ident[:]).then_inc(setup_done, 1)
            nc.vector.tensor_copy(ones_r[:], ones[:]).then_inc(setup_done, 1)
            dve.wait_ge(weights_in[0], 16 * WEIGHTS[0])
            for n in scaled_values:
                dve.wait_ge(weights_in[n], 16 * WEIGHTS[n])
                nc.vector.tensor_tensor(bv_col[n][:], bv_col[n][:], gamma_col[n][:], ALU.mult).then_inc(setup_done, 1)
                nc.vector.tensor_scalar(wv_sb[n][:], wv_sb[n][:], gamma_col[n][:], None, ALU.mult
                                        ).then_inc(setup_done, 1)
            dve.wait_ge(setup_done, SETUP)

            def part(i, u, job, layer):
                j = DEEP * i + u
                nxt, new, old = (u + 1) % DEEP, (u + 2) % DEEP, (u - 1) % DEEP

                def half_maximum(t, h):
                    if job(1):
                        n = h * MT + t
                        dve.wait_ge(rows_ready, (MT * (j + 1) + t) * HALVES + h + 1)
                        nc.vector.reduce_max(half_top[nxt % 2][:, n:n + 1], rows_ps[:, h * BANK:(h + 1) * BANK], AX_X,
                                             negate=True).then_inc(row_max, 1)

                def high_part(t):
                    if job(t // MT):
                        dve.wait_ge(probs_ready, (MT * j + t + 1) * HALVES)
                        positive(dve, probs_mixed, MT * j + t - PROBS + 1)
                        nc.vector.tensor_copy(probs_high[t % PROBS][:], probs[t % PROBS][:]).then_inc(high_ready, 1)

                def add_top():
                    if job(0):
                        dve.wait_ge(top_rows, j + 1)
                        rows = slice(64, P)
                        nc.vector.tensor_tensor(q[u % DEEP][rows, :], misc_ps[rows, :], q[u % DEEP][rows, :],
                                                ALU.add).then_inc(top_added, 1)

                def row_maxima():
                    if job(1):
                        tops, minus = top[nxt % 2], minus_top[nxt % 2]
                        dve.wait_ge(row_max, MT * (j + 2) * HALVES)
                        nc.vector.tensor_tensor(tops[:], half_top[nxt % 2][:, 0:MT], half_top[nxt % 2][:, MT:], ALU.min
                                                ).then_inc(top_ready, 1)
                        dve.wait_ge(top_ready, j + 2)
                        positive(dve, top_rows, j)
                        nc.vector.tensor_copy(minus[:, :, HIGH_ROW], tops[:]).then_inc(top_high, 1)
                        dve.wait_ge(top_high, j + 2)
                        nc.vector.tensor_tensor(minus[:, :, LOW_ROW], tops[:], minus[:, :, HIGH_ROW],
                                                ALU.subtract).then_inc(top_low, 1)

                def top_difference():
                    if job(0):
                        positive(dve, rescale_turn, 3 * j)
                        for h in range(HALVES):
                            n = slice(h * MT, (h + 1) * MT)
                            ins = nc.vector.tensor_tensor(rescale[:, n], top[u % 2][:], half_top[u % 2][:, n],
                                                          ALU.subtract)
                        ins.then_inc(rescale_turn, 1)

                def invert_sums():
                    if job(0):
                        dve.wait_ge(rescale_turn, 3 * j + 2)
                        nc.vector.tensor_tensor(rescale[:], rescale[:], half_sum[u % 2][:], ALU.mult
                                                ).then_inc(rescale_turn, 1)
                        dve.wait_ge(rescale_turn, 3 * j + 3)
                        nc.vector.tensor_tensor(row_sum[:], rescale[:, 0:MT], rescale[:, MT:], ALU.add
                                                ).then_inc(share_ready, 1)
                        dve.wait_ge(share_ready, 4 * j + 1)
                        nc.vector.reciprocal(share[:], row_sum[:]).then_inc(share_ready, 1)
                        dve.wait_ge(share_ready, 4 * j + 2)
                        positive(dve, diagonal_ready, 2 * j)
                        nc.vector.tensor_copy(share_high[:], share[:]).then_inc(share_ready, 1)
                        dve.wait_ge(share_ready, 4 * j + 3)
                        nc.vector.tensor_tensor(share_low[:], share[:], share_high[:], ALU.subtract
                                                ).then_inc(share_ready, 1)

                def keys_low_part():
                    if job(2):
                        low_part(k, slice(32, 64), bk_rows[layer(2)], k_high, k_low)

                def queries_low_part():
                    if job(2):
                        low_part(q, slice(64, 96), bq_rows[layer(2)], q_high, q_low)

                def values_low_part():
                    if job(2):
                        dve.wait_ge(v_ready, j + 3)
                        nc.vector.tensor_tensor(v_low[new][:], misc_ps[:], v_high[new][:],
                                                ALU.subtract).then_inc(v_low_ready, 1)

                def scale():
                    if job(-1):
                        dve.wait_ge(share_rows, j)
                        dve.wait_ge(mix_copied, j)
                        positive(dve, out_ready, j - 1)
                        nc.vector.tensor_tensor(scaled[:], misc_ps[:], mixed[old % 2][:], ALU.mult
                                                ).then_inc(scaled_ready, 1)

                def output():
                    if job(-1):
                        dve.wait_ge(scaled_ready, j)
                        stores = 16 * ((DEEP // 2) * i + (u - 1) // 2)
                        positive(dve, out_stored[old % 2], stores)
                        nc.vector.scalar_tensor_tensor(out[old % 2][:], scaled[:], bv_col[layer(-1)][:], x[old][:],
                                                       ALU.add, ALU.add).then_inc(out_ready, 1)

                def low_part(to, rows, bias, high, done):
                    dve.wait_ge(high, j + 3)
                    nc.vector.scalar_tensor_tensor(to[new][rows, :], misc_ps[rows, :], bias[rows, :],
                                                   to[new][rows, :], ALU.add, ALU.subtract).then_inc(done, 1)

                half_maximum(0, 0)
                half_maximum(0, 1)
                high_part(-3)
                add_top()
                top_difference()

                half_maximum(1, 0)
                half_maximum(1, 1)
                high_part(-2)

                half_maximum(2, 0)
                high_part(-1)
                half_maximum(2, 1)
                keys_low_part()

                half_maximum(3, 0)
                half_maximum(3, 1)
                high_part(0)
                invert_sums()

                high_part(1)
                half_maximum(4, 0)
                half_maximum(4, 1)
                queries_low_part()

                half_maximum(5, 0)
                half_maximum(5, 1)
                scale()
                high_part(2)

                high_part(3)
                half_maximum(6, 0)
                half_maximum(6, 1)
                output()

                half_maximum(7, 0)
                half_maximum(7, 1)
                high_part(4)
                row_maxima()
                values_low_part()

            pipeline(dve, part)

        @block.scalar
        def _(act):
            act.wait_ge(weights_in[0], 16 * WEIGHTS[0])
            act.wait_ge(setup_done, SETUP)

            def part(i, u, job, layer):
                j = DEEP * i + u
                new = (u + 2) % DEEP

                def exponentials(t, h):
                    if not job(t // MT):
                        return
                    act.wait_ge(keys_ready, (MT * j + t) * HALVES + h + 1)
                    if h == 0:
                        positive(act, low_ready, MT * j + t - PROBS + 1)
                    half = slice(h * BANK, (h + 1) * BANK)
                    nc.scalar.activation(probs[t % PROBS][:, half], keys_ps[:, half], ACT.Exp).then_inc(probs_ready, 1)

                def half_sums(t, h):
                    if job(1):
                        n = h * MT + t
                        act.wait_ge(row_max, (MT * (j + 1) + t) * HALVES + h + 1)
                        nc.scalar.activation(row_probs[:, h * BANK:(h + 1) * BANK], rows_ps[:, h * BANK:(h + 1) * BANK],
                                             ACT.Exp, bias=half_top[(u + 1) % 2][:, n:n + 1],
                                             accum_out=half_sum[(u + 1) % 2][:, n:n + 1]).then_inc(row_summed, 1)

                def rescale_halves():
                    if job(0):
                        act.wait_ge(rescale_turn, 3 * j + 1)
                        nc.scalar.activation(rescale[:], rescale[:], ACT.Exp).then_inc(rescale_turn, 1)

                def copy_mix():
                    if job(-1):
                        act.wait_ge(probs_mixed, MT * j)
                        positive(act, scaled_ready, j - 2)
                        nc.scalar.activation(mixed[(u - 1) % 2][:], mix_ps[:], ACT.Copy).then_inc(mix_copied, 1)

                def keys_high():
                    if job(2):
                        act.wait_ge(k_proj, j + 3)
                        nc.scalar.activation(k[new][:], misc_ps[:], ACT.Identity, bias=bk_rows[layer(2)][:]).then_inc(k_high, 1)

                def queries_high():
                    if job(2):
                        act.wait_ge(q_proj, j + 3)
                        nc.scalar.activation(q[new][:], misc_ps[:], ACT.Identity, bias=bq_rows[layer(2)][:]).then_inc(q_high, 1)

                def values_high():
                    if job(2):
                        act.wait_ge(v_proj, j + 3)
                        nc.scalar.activation(v_high[new][:], misc_ps[:], ACT.Copy).then_inc(v_ready, 1)

                exponentials(-2, 0)
                exponentials(-2, 1)
                half_sums(0, 0)
                half_sums(0, 1)

                exponentials(-1, 0)
                exponentials(-1, 1)
                rescale_halves()
                half_sums(1, 0)
                half_sums(1, 1)

                keys_high()
                exponentials(0, 0)
                exponentials(0, 1)
                half_sums(2, 0)
                half_sums(2, 1)

                exponentials(1, 0)
                exponentials(1, 1)
                half_sums(3, 0)
                half_sums(3, 1)

                queries_high()
                exponentials(2, 0)
                exponentials(2, 1)
                half_sums(4, 0)
                half_sums(4, 1)
                copy_mix()

                exponentials(3, 0)
                half_sums(5, 0)
                exponentials(3, 1)
                half_sums(5, 1)

                exponentials(4, 0)
                exponentials(4, 1)
                half_sums(6, 0)
                half_sums(6, 1)

                exponentials(5, 0)
                exponentials(5, 1)
                values_high()
                half_sums(7, 0)
                half_sums(7, 1)

            pipeline(act, part)

        @block.tensor
        def _(pe):
            pe.wait_ge(weights_in[0], 16 * WEIGHTS[0])
            pe.wait_ge(setup_done, SETUP)

            def part(i, u, job, layer):
                j = DEEP * i + u
                nxt, new, old = (u + 1) % DEEP, (u + 2) % DEEP, (u - 1) % DEEP

                def key_energies(t, h):
                    if not job(t // MT):
                        return
                    image, m = (u + t // MT) % DEEP, t % MT
                    if t == 0 and h == 0:
                        pe.wait_ge(top_added, j + 1)
                    half = slice(h * BANK, (h + 1) * BANK)
                    positive(pe, probs_ready, (MT * j + t - 1) * HALVES + h + 1)
                    nc.tensor.matmul(keys_ps[:, half], k[image][:, m * P:(m + 1) * P], q[image][:, half],
                                     start=True, stop=True).then_inc(keys_ready, 1)

                def row_energies(t, h):
                    if not job(1):
                        return
                    if t == 0 and h == 0:
                        pe.wait_ge(k_low, j + 2)
                        pe.wait_ge(q_low, j + 2)
                    half = slice(h * BANK, (h + 1) * BANK)
                    positive(pe, row_summed, (MT * (j + 1) + t - 1) * HALVES + h + 1)
                    nc.tensor.matmul(rows_ps[:, half], q[nxt][:, t * P:(t + 1) * P], k[nxt][:, half],
                                     start=True, stop=True).then_inc(rows_ready, 1)

                def mix(t, h):
                    if not job(t // MT):
                        return
                    image, m = (u + t // MT) % DEEP, t % MT
                    if m == 0 and h == 0:
                        pe.wait_ge(v_low_ready, j + 1)
                        positive(pe, mix_copied, j)
                    half, tile = slice(h * BANK, (h + 1) * BANK), slice(m * P, (m + 1) * P)
                    pe.wait_ge(high_ready, MT * j + t + 1)
                    for part in (v_high, v_low):
                        nc.tensor.matmul(mix_ps[:, half], part[image][:, tile], probs_high[t % PROBS][:, half],
                                         start=(m == 0 and part is v_high), stop=False)
                    pe.wait_ge(low_ready, MT * j + t + 1)
                    mm = nc.tensor.matmul(mix_ps[:, half], v_high[image][:, tile], probs_low[t % PROBS][:, half],
                                          start=False, stop=(m == MT - 1))
                    if h == HALVES - 1:
                        mm.then_inc(probs_mixed, 1)

                def project(weights, done):
                    for h in range(HALVES):
                        half = slice(h * BANK, (h + 1) * BANK)
                        mm = nc.tensor.matmul(misc_ps[:, half], weights[:], x[new][:, half], start=True, stop=True)
                    mm.then_inc(done, 1)

                def spread_shares():
                    if not job(-1):
                        return
                    pe.wait_ge(diagonal_ready, 2 * j)
                    if job(2):
                        pe.wait_ge(q_low, j + 3)
                    if job(0):
                        pe.wait_ge(top_added, j + 1)
                    positive(pe, scaled_ready, j - 1)
                    for h in range(HALVES):
                        half = slice(h * BANK, (h + 1) * BANK)
                        nc.tensor.matmul(misc_ps[:, half], ones_r[:], high_diagonal[old % 2][:, half],
                                         start=True, stop=False)
                        mm = nc.tensor.matmul(misc_ps[:, half], ones_r[:], low_diagonal[old % 2][:, half],
                                              start=False, stop=True)
                    mm.then_inc(share_rows, 1)

                def project_k():
                    if job(2):
                        pe.wait_ge(x_in[new], 16 * i + 16 * ((u + 2) // DEEP + 1))
                        positive(pe, v_low_ready, j + 2)
                        positive(pe, top_added, j + 1)
                        project(wk_rows[layer(2)], k_proj)

                def project_q():
                    if job(2):
                        pe.wait_ge(k_low, j + 3)
                        project(wq_rows[layer(2)], q_proj)

                def project_v():
                    if job(2):
                        positive(pe, scaled_ready, j)
                        pe.wait_ge(q_low, j + 3)
                        for t in range(MT):
                            mm = nc.tensor.matmul(misc_ps[:, t * P:(t + 1) * P], x[new][:, t * P:(t + 1) * P],
                                                  wv_sb[layer(2)][:], start=True, stop=True)
                        mm.then_inc(v_proj, 1)

                def spread_maxima():
                    if not job(0):
                        return
                    pe.wait_ge(top_low, j + 1)
                    if job(1):
                        pe.wait_ge(v_low_ready, j + 2)
                    positive(pe, scaled_ready, j - 1)
                    for t in range(MT):
                        mm = nc.tensor.matmul(misc_ps[:, t * P:(t + 1) * P], minus_top[u % 2][:, t, :], ident_r[:],
                                              start=True, stop=True)
                    mm.then_inc(top_rows, 1)

                key_energies(-2, 0)
                row_energies(0, 0)
                key_energies(-2, 1)
                mix(-5, 0)
                row_energies(0, 1)
                spread_maxima()
                mix(-5, 1)

                key_energies(-1, 0)
                row_energies(1, 0)
                key_energies(-1, 1)
                row_energies(1, 1)
                mix(-4, 0)
                project_k()

                key_energies(0, 0)
                key_energies(0, 1)
                row_energies(2, 0)
                mix(-4, 1)
                row_energies(2, 1)
                mix(-3, 0)
                mix(-3, 1)

                key_energies(1, 0)
                key_energies(1, 1)
                row_energies(3, 0)
                mix(-2, 0)
                row_energies(3, 1)
                project_q()

                key_energies(2, 0)
                row_energies(4, 0)
                key_energies(2, 1)
                row_energies(4, 1)
                mix(-2, 1)
                mix(-1, 0)
                mix(-1, 1)

                row_energies(5, 0)
                key_energies(3, 0)
                key_energies(3, 1)
                row_energies(5, 1)
                spread_shares()
                mix(0, 0)
                mix(0, 1)

                key_energies(4, 0)
                row_energies(6, 0)
                key_energies(4, 1)
                row_energies(6, 1)
                project_v()
                mix(1, 0)

                key_energies(5, 0)
                row_energies(7, 0)
                key_energies(5, 1)
                row_energies(7, 1)
                mix(1, 1)
                mix(2, 0)
                mix(2, 1)

            pipeline(pe, part)


def build(nc, t):
    with ExitStack() as ctx:
        psum = [ctx.enter_context(nc.psum_tensor(f"psum{n}", [P, CELLS], F32)) for n in range(4)]
        layers(nc, ctx, psum, t)


def layers(nc, sems, psum, t):
    inner = [nc.dram_tensor(f"layer{n}_out", [BATCH, P, CELLS], F32, kind="Internal").ap() for n in range(3)]
    scan_layer(nc, sems, "L0", psum, t["x_cells"], inner[0], *(t[f"L0_conv_{n}"] for n in ("w1", "b1", "w2", "b2", "w_y")))
    attention_layers(nc, sems, "L12", psum, inner,
                     [[t[f"L1_conv_{n}"] for n in ("Wq", "bq", "Wk", "bk", "Wv", "bv", "gamma")],
                      [t[f"L2_conv_{n}"] for n in ("wq", "bq", "wk", "bk", "wv", "bv")] + [None]])
    scan_layer(nc, sems, "L3", psum, inner[2], t["y_cells"], *(t[f"L3_conv_{n}"] for n in ("w1", "b1", "w2", "b2", "w_y")))


def kernel(**inputs):
    import concourse.bacc as bacc
    from concourse.bass_utils import run_bass_kernel_spmd

    arrays = {n: np.asarray(a) for n, a in inputs.items()}
    x = arrays.pop("x").reshape(BATCH, CELLS, P)[:, GRID, :]
    arrays["x_cells"] = np.ascontiguousarray(x.transpose(0, 2, 1))
    for n in ("L0_conv_b2", "L3_conv_b2", "L1_conv_gamma"):
        arrays[n] = arrays[n].reshape(1, 1)
    nc = bacc.Bacc("TRN2", target_bir_lowering=False, num_devices=1)
    t = {n: nc.dram_tensor(n, a.shape, F32, kind="ExternalInput").ap() for n, a in arrays.items()}
    t["y_cells"] = nc.dram_tensor("y_cells", [BATCH, P, CELLS], F32, kind="ExternalOutput").ap()
    build(nc, t)
    got = run_bass_kernel_spmd(nc, [arrays], core_ids=[0]).results[0]["y_cells"]
    y = np.empty((BATCH, CELLS, P), np.float32)
    y[:, GRID, :] = got.transpose(0, 2, 1)
    return y.reshape(BATCH, SIDE, SIDE, P)
```
